# Optimizing a Trainium2 kernel written in Bass

```python
import numpy as np
import jax
import jax.numpy as jnp

def _softmax(x, axis=-1):
    return jax.nn.softmax(x, axis=axis)

def _gelu(x):
    return jax.nn.gelu(x, approximate=True)

def _silu(x):
    return jax.nn.silu(x)

def _sigmoid(x):
    return jax.nn.sigmoid(x)

def _layernorm(x, axis=-1, eps=1e-05):
    m = jnp.mean(x, axis=axis, keepdims=True)
    v = jnp.var(x, axis=axis, keepdims=True)
    return (x - m) / jnp.sqrt(v + eps)

def _scatter_add(tgt, idx, src, axis=0):
    return tgt.at[idx].add(src)

def _segment_sum(src, seg, n):
    return jax.ops.segment_sum(src, seg, n)
kernel_name = 'mk_seq_postln_d1_jaxref_r4_ed1e14'

def setup_inputs(seed: int=0):
    np.random.seed(seed)
    _w = jnp.asarray

    def _L0_attn_setup():
        import jax, jax.numpy as jnp
        import numpy as np
        B, T, D, H = (4, 512, 256, 16)
        HEAD_DIM = D // H
        LOCAL_WINDOW = 128

        def _rotate_half(t):
            t1, t2 = jnp.split(t, 2, axis=-1)
            return jnp.concatenate([-t2, t1], axis=-1)

        def _apply_rope(q, k):
            Tq, d = (q.shape[2], q.shape[3])
            half = d // 2
            theta = 1.0 / 10000.0 ** (jnp.arange(half, dtype=jnp.float32) / half)
            pos = jnp.arange(Tq, dtype=jnp.float32)
            freqs = pos[:, None] * theta[None, :]
            freqs = jnp.concatenate([freqs, freqs], axis=-1)
            cos = jnp.cos(freqs)[None, None]
            sin = jnp.sin(freqs)[None, None]
            q = q * cos + _rotate_half(q) * sin
            k = k * cos + _rotate_half(k) * sin
            return (q, k)
        key = jax.random.key(seed)
        k1, k2, k3 = jax.random.split(key, 3)
        x = jax.random.normal(k1, (B, T, D), dtype=jnp.float32)
        Wqkv = jax.random.normal(k2, (D, 3 * D), dtype=jnp.float32) * 0.02
        Wout = jax.random.normal(k3, (D, D), dtype=jnp.float32) * 0.02
        return {'x': x, 'Wqkv': Wqkv, 'Wout': Wout}
    _L0_attn_in = _L0_attn_setup()

    def _L0_ffn_setup():
        import jax, jax.numpy as jnp
        import numpy as np
        D_IN, D_HID = (256, 1024)

        def _ternary(key, shape):
            return jax.random.randint(key, shape, -1, 2).astype(jnp.float32)

        def _tlin(x, w, s):
            return jnp.einsum('bsi,oi->bso', x, w) * s
        key = jax.random.key(seed)
        ks = jax.random.split(key, 12)
        inv = lambda fan: 1.0 / np.sqrt(fan).astype(np.float32)
        return {'x': jax.random.normal(ks[0], (4, 512, D_IN), dtype=jnp.float32), 'w1_w': _ternary(ks[1], (D_HID, D_IN)), 'w1_s': jax.random.uniform(ks[2], (D_HID,), dtype=jnp.float32) * inv(D_IN), 'w2_w': _ternary(ks[3], (D_HID, D_IN)), 'w2_s': jax.random.uniform(ks[4], (D_HID,), dtype=jnp.float32) * inv(D_IN), 'h1_w': _ternary(ks[5], (D_HID, D_HID)), 'h1_s': jax.random.uniform(ks[6], (D_HID,), dtype=jnp.float32) * inv(D_HID), 'h2_w': _ternary(ks[7], (D_HID, D_HID)), 'h2_s': jax.random.uniform(ks[8], (D_HID,), dtype=jnp.float32) * inv(D_HID), 'w3_w': _ternary(ks[9], (D_IN, D_HID)), 'w3_s': jax.random.uniform(ks[10], (D_IN,), dtype=jnp.float32) * inv(D_HID)}
    _L0_ffn_in = _L0_ffn_setup()
    _d = {'L0_attn_x': _L0_attn_in['x'], 'L0_attn_Wqkv': _L0_attn_in['Wqkv'], 'L0_attn_Wout': _L0_attn_in['Wout'], 'L0_ffn_w1_w': _L0_ffn_in['w1_w'], 'L0_ffn_w1_s': _L0_ffn_in['w1_s'], 'L0_ffn_w2_w': _L0_ffn_in['w2_w'], 'L0_ffn_w2_s': _L0_ffn_in['w2_s'], 'L0_ffn_h1_w': _L0_ffn_in['h1_w'], 'L0_ffn_h1_s': _L0_ffn_in['h1_s'], 'L0_ffn_h2_w': _L0_ffn_in['h2_w'], 'L0_ffn_h2_s': _L0_ffn_in['h2_s'], 'L0_ffn_w3_w': _L0_ffn_in['w3_w'], 'L0_ffn_w3_s': _L0_ffn_in['w3_s']}
    _x0 = _d['L0_attn_x']
    _d['L0_attn_x'] = jax.random.normal(jax.random.fold_in(jax.random.key(seed), 1), (8, 512, 256), dtype=_x0.dtype)
    del _x0
    return _d

def reference(L0_attn_x, L0_attn_Wqkv, L0_attn_Wout, L0_ffn_w1_w, L0_ffn_w1_s, L0_ffn_w2_w, L0_ffn_w2_s, L0_ffn_h1_w, L0_ffn_h1_s, L0_ffn_h2_w, L0_ffn_h2_s, L0_ffn_w3_w, L0_ffn_w3_s):

    def _L0_attn_ref(x, Wqkv, Wout):
        import jax, jax.numpy as jnp
        import numpy as np
        B, T, D, H = (4, 512, 256, 16)
        HEAD_DIM = D // H
        LOCAL_WINDOW = 128

        def _rotate_half(t):
            t1, t2 = jnp.split(t, 2, axis=-1)
            return jnp.concatenate([-t2, t1], axis=-1)

        def _apply_rope(q, k):
            Tq, d = (q.shape[2], q.shape[3])
            half = d // 2
            theta = 1.0 / 10000.0 ** (jnp.arange(half, dtype=jnp.float32) / half)
            pos = jnp.arange(Tq, dtype=jnp.float32)
            freqs = pos[:, None] * theta[None, :]
            freqs = jnp.concatenate([freqs, freqs], axis=-1)
            cos = jnp.cos(freqs)[None, None]
            sin = jnp.sin(freqs)[None, None]
            q = q * cos + _rotate_half(q) * sin
            k = k * cos + _rotate_half(k) * sin
            return (q, k)
        Bx, Tx, C = x.shape
        h, d, w = (H, HEAD_DIM, LOCAL_WINDOW)
        qkv = x @ Wqkv
        q, k, v = jnp.split(qkv, 3, axis=-1)
        q = q.reshape(Bx, Tx, h, d).transpose(0, 2, 1, 3)
        k = k.reshape(Bx, Tx, h, d).transpose(0, 2, 1, 3)
        v = v.reshape(Bx, Tx, h, d).transpose(0, 2, 1, 3)
        q, k = _apply_rope(q, k)
        idx = jnp.arange(Tx)
        dist = idx[None, :] - idx[:, None]
        allowed = (dist <= 0) & (dist >= -(w - 1))
        scores = jnp.einsum('bhqd,bhkd->bhqk', q, k) / jnp.sqrt(jnp.float32(d))
        scores = jnp.where(allowed[None, None], scores, -jnp.inf)
        weights = jax.nn.softmax(scores, axis=-1)
        out = jnp.einsum('bhqk,bhkd->bhqd', weights, v)
        out = out.transpose(0, 2, 1, 3).reshape(Bx, Tx, C)
        return out @ Wout

    def _L0_ffn_ref(x, w1_w, w1_s, w2_w, w2_s, h1_w, h1_s, h2_w, h2_s, w3_w, w3_s):
        import jax, jax.numpy as jnp
        import numpy as np
        D_IN, D_HID = (256, 1024)

        def _ternary(key, shape):
            return jax.random.randint(key, shape, -1, 2).astype(jnp.float32)

        def _tlin(x, w, s):
            return jnp.einsum('bsi,oi->bso', x, w) * s
        h = jax.nn.silu(_tlin(x, w1_w, w1_s)) * _tlin(x, w2_w, w2_s)
        h = jax.nn.gelu(_tlin(h, h1_w, h1_s), approximate=False)
        h = jax.nn.gelu(_tlin(h, h2_w, h2_s), approximate=False)
        return _tlin(h, w3_w, w3_s)
    x = L0_attn_x
    x = _layernorm(x + _L0_attn_ref(x, L0_attn_Wqkv, L0_attn_Wout), axis=-1)
    x = _layernorm(x + _L0_ffn_ref(x, L0_ffn_w1_w, L0_ffn_w1_s, L0_ffn_w2_w, L0_ffn_w2_s, L0_ffn_h1_w, L0_ffn_h1_s, L0_ffn_h2_w, L0_ffn_h2_s, L0_ffn_w3_w, L0_ffn_w3_s), axis=-1)
    return x

_drawn_inputs = setup_inputs


def setup_inputs(seed=0):
    import zlib

    import numpy as np

    out = dict(_drawn_inputs(seed))
    spreads = {}
    factors = {'L0_attn_Wqkv': 4.269,
     'L0_attn_Wout': 4.309,
     'L0_ffn_w1_w': 8.0,
     'L0_ffn_w1_s': 8.0,
     'L0_ffn_w2_w': 8.0,
     'L0_ffn_w2_s': 8.0,
     'L0_ffn_h1_w': 8.0,
     'L0_ffn_h1_s': 8.0,
     'L0_ffn_h2_w': 8.0,
     'L0_ffn_h2_s': 8.0,
     'L0_ffn_w3_w': 8.0,
     'L0_ffn_w3_s': 8.0}
    for name, (base, spread) in spreads.items():
        noise = np.random.default_rng([zlib.crc32(name.encode()), seed]).standard_normal(out[name].shape)
        drawn = base * np.exp(spread * noise) if base else spread * noise
        out[name] = jnp.asarray(drawn.astype(out[name].dtype))
    for name, factor in factors.items():
        out[name] = (out[name] * factor).astype(out[name].dtype)
    return out
```

```python
from contextlib import ExitStack

import numpy as np

import concourse.bass as bass
from concourse import mybir

ALU = mybir.AluOpType
ACT = mybir.ActivationFunctionType
AX = mybir.AxisListType
F32 = mybir.dt.float32
F32R = mybir.dt.float32r
U8 = mybir.dt.uint8

P = 128
NB = 8
TB = 512
NT = TB // P
D = 256
KD = D // P
H = 16
HD = D // H
HALF = HD // 2
HID = 1024
KH = HID // P
WINDOW = 128
EPS = 1e-5

GH = 4
NG = H // GH
STEPS = NG * NT
SLOT = 64
PARTS = 3 * HD
NST = 4
MASKED = 3e38
GLU_COLS = 2 * KD * P
HID_COLS = KH * P
W3_COLS = D
PACK = GLU_COLS + 2 * HID_COLS + W3_COLS
NPIECE = 4
PIECE = PACK // NPIECE

QKV_STEP = {1: 0, 3: 1, 7: 2, 10: 3}
STACK_STEP = {s: [s - 3] for s in range(3, 14)} | {14: [11, 12], 15: [13]}
LATE_STACK = {0: [14], 1: [15]}
SHARED_STEPS = (3, 4, 5, 7, 8, 9, 11, 12, 13, 15)
LAST_SHARED_STEPS = (3, 4, 5, 8, 9, 12, 13)


def shared_uses(b, s, first, flush):
    if first:
        return {7: 0, 11: 1, 15: 2}[s]
    before_block = len(SHARED_STEPS) * b - 7
    if flush:
        return before_block + LAST_SHARED_STEPS.index(s)
    return before_block + SHARED_STEPS.index(s)


def wait_count(eng, sem, count):
    if not isinstance(count, int) or count > 0:
        eng.wait_ge(sem, count)


def over_blocks(eng, block):
    block(0, 0, True, False)
    with eng.Fori(0, (NB - 2) // 2) as pair:
        for j in (1, 2):
            block(pair * 2 + j, j % 2, False, False)
    block(NB - 1, (NB - 1) % 2, False, True)


def build(nc, x, xT, wqkv, wout, wffn, s1, s2, sh1, sh2, s3, cos, sin, lower, upper, bias, ident, out):
    x_v = x.rearrange("(b t p) d -> b p t d", b=NB, t=NT)
    out_v = out.rearrange("(b t p) d -> b p t d", b=NB, t=NT)
    with ExitStack() as ctx:
        def scratch(name, shape, dt=F32):
            return nc.dram_tensor(name, shape, dt, kind="Internal").ap()

        w_hi_d = scratch("w_hi_d", (NB, P, PACK))
        w_lo_d = scratch("w_lo_d", (NB, P, PACK))
        x1_d = scratch("x1_d", (NB, P, NT, D))
        x1T_d = scratch("x1T_d", (NB, P, KD, TB))
        h1_d = scratch("h1_d", (NB, P, KH, TB))

        base = (nc.sbuf_base + 63) // 64 * 64
        cursor = [base]

        def sb(name, shape, dt=F32):
            size = int(np.prod(shape[1:])) * (1 if dt == U8 else 4)
            at = cursor[0]
            cursor[0] += (size + 31) // 32 * 32
            return nc.alloc_sbuf_tensor_at(name, shape, dt, offset=at)

        def bank(name):
            return ctx.enter_context(nc.psum_tensor(name, [P, 512], F32))

        def sem(name):
            return ctx.enter_context(nc.semaphore(name))

        s1_s, s2_s, sh1_s, sh2_s = (sb(n, [P, KH]) for n in ("s1_s", "s2_s", "sh1_s", "sh2_s"))
        s3_s = sb("s3_s", [P, KD])
        ident_s = sb("ident_s", [P, P])
        neg_half = sb("neg_half", [P, 4])
        stats = sb("stats", [P, 4, 6])
        meanvar = sb("meanvar", [P, 4, 2])
        vareps, rstd0, rsq, rstd = (sb(n, [P, 4]) for n in ("vareps", "rstd0", "rsq", "rstd"))
        phase_base = cursor[0]

        ident_r = sb("ident_r", [P, P], F32R)
        wq_hi, wq_lo = sb("wq_hi", [P, KD, 3 * D], F32R), sb("wq_lo", [P, KD, 3 * D], F32R)
        wo_hi, wo_lo = sb("wo_hi", [P, KD, D], F32R), sb("wo_lo", [P, KD, D], F32R)
        qT = [sb(f"qT{i}", [P, H // 2, TB], F32R) for i in range(2)]
        kT = [sb(f"kT{i}", [P, H // 2, TB], F32R) for i in range(2)]
        v_s = [sb(f"v{i}", [P, NT, H, 2 * HD]) for i in range(2)]
        stack = [sb(f"stack{i}", [P, 2 * H, 4, HD], F32R) for i in range(2)]
        xT_s = sb("xT_s", [P, KD, TB])
        xT_hi, xT_lo = sb("xT_hi", [P, KD, TB], F32R), sb("xT_lo", [P, KD, TB], F32R)
        x_s = [sb(f"x_s{i}", [P, NT, D]) for i in range(2)]
        rope_a, rope_b = sb("rope_a", [P, 2 * D]), sb("rope_b", [P, 2 * D])
        qk_s = [sb(f"qk_s{i}", [P, 2 * D]) for i in range(2)]
        merged_s = [sb(f"merged_s{i}", [P, GH, P]) for i in range(2)]
        low = [sb(f"low{i}", [P, GH]) for i in range(2)]
        prob = [sb(f"prob{i}", [P, GH, P]) for i in range(2)]
        probT = [sb(f"probT{i}", [P, GH, 2 * P]) for i in range(2)]
        headT = sb("headT", [P, TB])
        denom = sb("denom", [P, NT, GH])
        att = sb("att", [P, NT, D])
        attT_hi, attT_lo = sb("attT_hi", [P, KD, TB], F32R), sb("attT_lo", [P, KD, TB], F32R)
        res = sb("res", [P, NT, D])
        x1T_s = sb("x1T_s", [P, KD, TB])
        cos_s, sin_s, nsin_s = (sb(n, [P, NT, 2, HALF]) for n in ("cos_s", "sin_s", "nsin_s"))
        lower_s, upper_s, bias_s = (sb(n, [P, P]) for n in ("lower_s", "upper_s", "bias_s"))
        take_s = sb("take_s", [P, P], U8)
        piece = sb("piece", [P, PIECE])
        piece_hi, piece_lo = sb("piece_hi", [P, PIECE], F32R), sb("piece_lo", [P, PIECE], F32R)
        a_end = cursor[0]
        wq_f = nc.alloc_sbuf_tensor_at("wq_f", [P, KD, 3 * D], F32, offset=a_end)
        wo_f = nc.alloc_sbuf_tensor_at("wo_f", [P, KD, D], F32, offset=a_end + 4 * KD * 3 * D)
        a_end += 4 * KD * 4 * D

        cursor[0] = phase_base
        wh2_hi = sb("wh2_hi", [P, KH, HID_COLS], F32R)
        bc_base = cursor[0]
        wglu_hi, wglu_lo = sb("wglu_hi", [P, KH, GLU_COLS], F32R), sb("wglu_lo", [P, KH, GLU_COLS], F32R)
        after_glu = cursor[0]
        wh1_hi, wh1_lo = sb("wh1_hi", [P, KH, HID_COLS], F32R), sb("wh1_lo", [P, KH, HID_COLS], F32R)
        after_h1w = cursor[0]
        bx_s = sb("bx_s", [P, KD, TB])
        bx_hi, bx_lo = sb("bx_hi", [P, KD, TB], F32R), sb("bx_lo", [P, KD, TB], F32R)
        after_bx = cursor[0] = max(cursor[0], after_h1w + 2 * 4 * KH * D)
        h0_hi, h0_lo = sb("h0_hi", [P, KH, TB], F32R), sb("h0_lo", [P, KH, TB], F32R)
        silu_s = [sb(f"silu_s{i}", [P, TB]) for i in range(2)]
        h0_s = [sb(f"h0_s{i}", [P, TB]) for i in range(2)]
        h1_s = [sb(f"h1_s{i}", [P, TB]) for i in range(2)]
        b_end = cursor[0]

        cursor[0] = bc_base
        wh2_lo = sb("wh2_lo", [P, KH, HID_COLS], F32R)
        assert cursor[0] <= after_glu
        cursor[0] = after_glu
        h1_hi = [sb(f"h1_hi{i}", [P, KH, TB], F32R) for i in range(2)]
        h1_lo = [sb(f"h1_lo{i}", [P, KH, TB], F32R) for i in range(2)]
        assert cursor[0] <= after_h1w
        cursor[0] = after_h1w
        w3_hi, w3_lo = sb("w3_hi", [P, KH, D], F32R), sb("w3_lo", [P, KH, D], F32R)
        assert cursor[0] <= after_bx
        cursor[0] = after_bx
        h1_in = [sb(f"h1_in{i}", [P, TB]) for i in range(4)]
        h2_s = [sb(f"h2_s{i}", [P, TB]) for i in range(2)]
        h2_hi = [sb(f"h2_hi{i}", [P, TB], F32R) for i in range(2)]
        h2_lo = [sb(f"h2_lo{i}", [P, TB], F32R) for i in range(2)]
        oT_s = sb("oT_s", [P, KD, TB])
        x1_s = sb("x1_s", [P, NT, D])
        y_s = sb("y_s", [P, NT, D])
        c_end = cursor[0]
        for end in (a_end, b_end, c_end):
            assert end <= nc.sbuf_usable_end, (a_end, b_end, c_end, nc.sbuf_usable_end)

        banks = [bank(f"bank{i}") for i in range(8)]
        ps_qk, ps_v, ps_stack = banks[0], banks[1], banks[2]
        ps_score = [banks[3], banks[4]]
        ps_probT, ps_head, ps_shared = banks[5], banks[6], banks[7]
        ps_stack_r = ps_stack[:, :].bitcast(F32R)
        ps_gate, ps_up, ps_h = [banks[0], banks[1]], [banks[2], banks[3]], [banks[4], banks[5]]
        ps_oT = [banks[2], banks[3]]
        ps_y = [banks[6], banks[7]]

        N_CONST = 12
        const_in = sem("const_in")
        wattn_in = sem("wattn_in")
        const_set = sem("const_set")
        wattn_hi = sem("wattn_hi")
        wattn_split = sem("wattn_split")
        xT_in, xT_hi_ready, xT_ready = sem("xT_in"), sem("xT_hi_ready"), sem("xT_ready")
        x_in = sem("x_in")
        qkv_done, qk_read, v_read = sem("qkv_done"), sem("qk_read"), sem("v_read")
        rope_terms, rope_sum = sem("rope_terms"), sem("rope_sum")
        stack_hi, stack_hi2, stack_lo = sem("stack_hi"), sem("stack_hi2"), sem("stack_lo")
        stackT_done, stackT_read = sem("stackT_done"), sem("stackT_read")
        score_done, copied, merged, low_ready = sem("score_done"), sem("copied"), sem("merged"), sem("low_ready")
        exp_done, probT_done, probT_read = sem("exp_done"), sem("probT_done"), sem("probT_read")
        head_done, head_read = sem("head_done"), sem("head_read")
        shared_done, shared_read, shared_hi = sem("shared_done"), sem("shared_read"), sem("shared_hi")
        denom_ready = sem("denom_ready")
        stats_ready, mean_ready, rstd_step, rstd_ready = (
            sem("stats_ready"), sem("mean_ready"), sem("rstd_step"), sem("rstd_ready"))
        x1_ready, x1_out, x1T_out = sem("x1_ready"), sem("x1_out"), sem("x1T_out")
        piece_in, piece_hi_ready, piece_lo_ready = sem("piece_in"), sem("piece_hi_ready"), sem("piece_lo_ready")
        piece_out = sem("piece_out")
        wb_in = [sem(f"wglu_in{m}") for m in range(KH)]
        wh1_in = [sem(f"wh1_in{m}") for m in range(KH)]
        bx_in, bx_hi_ready, bx_ready = sem("bx_in"), sem("bx_hi_ready"), sem("bx_ready")
        gate_done, up_done, silu_ready, h0_ready = (
            sem("gate_done"), sem("up_done"), sem("silu_ready"), sem("h0_ready"))
        h0_hi_ready, h0_split, h1_mm, h1_ready = sem("h0_hi_ready"), sem("h0_split"), sem("h1_mm"), sem("h1_ready")
        h1_out = [sem("h1_out0"), sem("h1_out1")]
        wh2_in = [sem(f"wh2_in{m}") for m in range(KH)]
        w3_in = sem("w3_in")
        h1_in_s = [sem(f"h1_in_s{i}") for i in range(4)]
        h1_hi_ready, h1_split = sem("h1_hi_ready"), sem("h1_split")
        h2_mm, h2_ready, h2_hi_ready, h2_split = sem("h2_mm"), sem("h2_ready"), sem("h2_hi_ready"), sem("h2_split")
        w3_done, oT_ready, yT_done, y_sum = sem("w3_done"), sem("oT_ready"), sem("yT_done"), sem("y_sum")
        cstats_ready, cmean_ready, crstd_step, crstd_ready = (
            sem("cstats_ready"), sem("cmean_ready"), sem("crstd_step"), sem("crstd_ready"))
        x1_in, y_ready, y_out = sem("x1_in"), sem("y_ready"), sem("y_out")

        block = ctx.enter_context(nc.Block())

        @block.sync
        def _(sp):
            sp.dma_start(xT_s[:], xT[0]).then_inc(xT_in, 16)
            sp.dma_start(wq_f[:], wqkv).then_inc(wattn_in, 16)
            sp.dma_start(wo_f[:], wout).then_inc(wattn_in, 16)
            for dst, src in ((ident_s, ident), (cos_s, cos), (sin_s, sin[0]), (nsin_s, sin[1]), (lower_s, lower),
                             (upper_s, upper), (bias_s, bias), (s1_s, s1), (s2_s, s2),
                             (sh1_s, sh1), (sh2_s, sh2), (s3_s, s3)):
                sp.dma_start(dst[:], src).then_inc(const_in, 16)

            def results(b, flush):
                sp.wait_ge(x1_ready, 2 * b + 2)
                sp.dma_start(x1_d[b], res[:]).then_inc(x1_out, 16)
                sp.wait_ge(shared_read, shared_uses(b + 1, 13, False, flush) + 1)
                sp.dma_start(x1T_d[b], x1T_s[:]).then_inc(x1T_out, 16)

            def phase_a(b, par, first, last):
                if not last:
                    sp.wait_ge(xT_ready, b + 1)
                    sp.dma_start(xT_s[:], xT[b + 1]).then_inc(xT_in, 16)
                wait_count(sp, x_in, 16 * b)
                sp.dma_start(x_s[par][:], x_v[b]).then_inc(x_in, 16)
                for q in range(NPIECE):
                    wait_count(sp, piece_lo_ready, NPIECE * b + q)
                    sp.dma_start(piece[:], wffn[b, :, q * PIECE:(q + 1) * PIECE]).then_inc(piece_in, 16)
                    sp.wait_ge(piece_lo_ready, NPIECE * b + q + 1)
                    sp.dma_start(w_hi_d[b, :, q * PIECE:(q + 1) * PIECE], piece_hi[:].bitcast(F32)).then_inc(piece_out, 16)
                    sp.dma_start(w_lo_d[b, :, q * PIECE:(q + 1) * PIECE], piece_lo[:].bitcast(F32)).then_inc(piece_out, 16)
                if not first:
                    results(b - 1, False)

            sp.sem_inc(x1_out, 16)
            sp.sem_inc(x1T_out, 16)
            sp.sem_inc(y_out, 16)
            over_blocks(sp, phase_a)
            results(NB - 1, True)

            sp.wait_ge(piece_out, 16 * 2 * NPIECE * NB)
            sp.wait_ge(x1T_out, 16 * (NB + 1))
            sp.wait_ge(x1_out, 16 * (NB + 1))
            sp.dma_start(bx_s[:], x1T_d[0]).then_inc(bx_in, 16)
            for m in range(KH):
                sp.dma_start(wglu_hi[:, m, :].bitcast(F32), w_hi_d[m, :, 0:GLU_COLS]).then_inc(wb_in[m], 16)
                sp.dma_start(wglu_lo[:, m, :].bitcast(F32), w_lo_d[m, :, 0:GLU_COLS]).then_inc(wb_in[m], 16)
            for m in range(KH):
                sp.dma_start(wh1_hi[:, m, :].bitcast(F32), w_hi_d[m, :, GLU_COLS:GLU_COLS + HID_COLS]).then_inc(wh1_in[m], 16)
                sp.dma_start(wh1_lo[:, m, :].bitcast(F32), w_lo_d[m, :, GLU_COLS:GLU_COLS + HID_COLS]).then_inc(wh1_in[m], 16)
            C2 = GLU_COLS + HID_COLS
            for m in range(KH):
                sp.dma_start(wh2_hi[:, m, :].bitcast(F32), w_hi_d[m, :, C2:C2 + HID_COLS]).then_inc(wh2_in[m], 16)

            def phase_b(b, load_next):
                if load_next:
                    sp.wait_ge(bx_ready, b + 1)
                    sp.dma_start(bx_s[:], x1T_d[b + 1]).then_inc(bx_in, 16)
                for m in range(KH):
                    sp.wait_ge(h1_ready, KH * b + m + 1)
                    sp.dma_start(h1_d[b, :, m, :], h1_s[m % 2][:]).then_inc(h1_out[m % 2], 16)

            with sp.Fori(0, NB - 1) as b:
                phase_b(b, True)
            sp.wait_ge(up_done, KH * NB)
            for m in range(KH):
                sp.dma_start(wh2_lo[:, m, :].bitcast(F32), w_lo_d[m, :, C2:C2 + HID_COLS]).then_inc(wh2_in[m], 16)
            C3 = C2 + HID_COLS
            for m in range(KH):
                sp.dma_start(w3_hi[:, m, :].bitcast(F32), w_hi_d[m, :, C3:PACK]).then_inc(w3_in, 16)
                sp.dma_start(w3_lo[:, m, :].bitcast(F32), w_lo_d[m, :, C3:PACK]).then_inc(w3_in, 16)
            phase_b(NB - 1, False)

            for i in range(2):
                sp.wait_ge(h1_out[i], 16 * NB * KH // 2)

            def load_h1(b, k):
                wait_count(sp, h1_split, KH * b + k - 3)
                sp.dma_start(h1_in[k % 4][:], h1_d[b, :, k, :]).then_inc(h1_in_s[k % 4], 16)

            def results_c(b):
                sp.wait_ge(y_ready, 2 * (b + 1))
                sp.dma_start(out_v[b], y_s[:]).then_inc(y_out, 16)

            for k in range(KH):
                load_h1(0, k)

            def phase_c(b, par, first, last):
                for k in range(KH):
                    if not last:
                        load_h1(b + 1, k)
                    if k == 5:
                        if not first:
                            results_c(b - 1)
                        wait_count(sp, y_sum, 2 * b)
                        sp.dma_start(x1_s[:], x1_d[b]).then_inc(x1_in, 16)

            over_blocks(sp, phase_c)
            results_c(NB - 1)
            sp.wait_ge(y_out, 16 * (NB + 1))

        @block.tensor
        def _(pe):
            def qkv(b, t):
                if t == 0:
                    pe.wait_ge(xT_ready, b + 1)
                wait_count(pe, qk_read, NT * b + t)
                wait_count(pe, v_read, NT * b + t)
                for kc in range(KD):
                    xh = xT_hi[:, kc, t * P:(t + 1) * P]
                    xl = xT_lo[:, kc, t * P:(t + 1) * P]
                    for n, (a, w) in enumerate(((xh, wq_hi), (xh, wq_lo), (xl, wq_hi))):
                        first, last = kc == 0 and n == 0, kc == KD - 1 and n == 2
                        pe.matmul(ps_qk[:, :], a, w[:, kc, 0:2 * D], start=first, stop=last)
                        mm = pe.matmul(ps_v[:, 0:D], a, w[:, kc, 2 * D:3 * D], start=first, stop=last)
                mm.then_inc(qkv_done, 1)

            def stack_transpose(b, g):
                t, part = g // NST, g % NST
                wait_count(pe, stackT_read, STEPS * b + g)
                pe.wait_ge(stack_lo, 2 * (NT * b + t + 1))
                pe.wait_ge(stack_hi2, 2 * (NT * b + t + 1))
                flat = stack[t % 2][:].rearrange("p h s d -> p (h s d)")
                at = (part % 2) * H * SLOT + (part // 2) * 4 * P
                for j in range(4):
                    mm = pe.transpose(ps_stack_r[:, j * P:(j + 1) * P], flat[:, at + j * P:at + (j + 1) * P],
                                      ident_r[:, :])
                mm.then_inc(stackT_done, 1)

            def scores(b, par, s):
                hg, i = s // NT, s % NT
                if hg in (0, 2):
                    if i == 0:
                        pe.wait_ge(stackT_read, NST * NT * b + (NST * NT - 2 if hg == 0 else NST * NT))
                k0 = max(i - 1, 0) * P
                for j in range(2):
                    hp = 2 * hg + j
                    for r in range(2):
                        if j == 0:
                            wait_count(pe, merged, 2 * (STEPS * b + s - 1) + r + 1)
                        lo = SLOT * r
                        mm = pe.matmul(ps_score[r][:, j * 2 * P:(j + 1) * 2 * P],
                                       qT[par][lo:lo + PARTS, hp, i * P:(i + 1) * P],
                                       kT[par][lo:lo + PARTS, hp, k0:k0 + 2 * P], start=True, stop=True)
                        if j == 1:
                            mm.then_inc(score_done, 1)

            def prob_transpose(b, s):
                wait_count(pe, probT_read, STEPS * b + s)
                pe.wait_ge(exp_done, STEPS * b + s + 1)
                for c in range(GH):
                    mm = pe.transpose(ps_probT[:, c * P:(c + 1) * P], prob[s % 2][:, c, :], ident_s[:, :])
                mm.then_inc(probT_done, 1)

            def weigh(b, par, s, j):
                hg = s // NT
                if j == 0:
                    wait_count(pe, head_read, NG * b + hg)
                n = 2 * P if j < NT - 1 else P
                for c in range(GH):
                    mm = pe.matmul(ps_head[32 * c:32 * c + 32, j * P:j * P + n], v_s[par][:, j, hg * GH + c, :],
                                   probT[j % 2][:, c, 0:n], start=(j == 0), stop=(j == NT - 1),
                                   skip_group_check=True)
                mm.then_inc(head_done, 1)

            def weigh_behind(b, par, s):
                i = s % NT
                if i >= 1:
                    pe.wait_ge(probT_read, STEPS * b + s + 1)
                    weigh(b, par, s, i - 1)
                if i == NT - 1:
                    weigh(b, par, s, i)

            def to_tokens(b, hg, no):
                pe.wait_ge(head_read, NG * b + hg + 1)
                wait_count(pe, shared_read, no)
                for t in range(NT):
                    mm = pe.transpose(ps_shared[:, t * P:(t + 1) * P], headT[:, t * P:(t + 1) * P], ident_s[:, :])
                mm.then_inc(shared_done, 1)

            def turn(src, kc, no):
                pe.wait_ge(shared_read, no)
                for t in range(NT):
                    mm = pe.transpose(ps_shared[:, t * P:(t + 1) * P], src[:, t, kc * P:(kc + 1) * P], ident_s[:, :])
                mm.then_inc(shared_done, 1)

            def project(pair, no):
                pe.wait_ge(shared_read, no)
                n = 0
                for u in range(2):
                    t = 2 * pair + u
                    for kc in range(KD):
                        ah, al = (a[:, kc, t * P:(t + 1) * P] for a in (attT_hi, attT_lo))
                        for a, w in ((ah, wo_hi), (ah, wo_lo), (al, wo_hi)):
                            mm = pe.matmul(ps_shared[:, u * D:(u + 1) * D], a, w[:, kc, :], start=(n == 0),
                                           stop=(n % 6 == 5), skip_group_check=True)
                            n += 1
                mm.then_inc(shared_done, 1)

            def shared(b, s, first, flush):
                if s not in SHARED_STEPS or (first and s not in (7, 11, 15)) or (flush and s not in LAST_SHARED_STEPS):
                    return
                no = shared_uses(b, s, first, flush)
                if s % 4 == 3:
                    if s == 3:
                        to_tokens(b - 1, NG - 1, no)
                    else:
                        to_tokens(b, s // 4 - 1, no)
                elif s in (4, 5):
                    turn(att, s - 4, no)
                elif s in (8, 9):
                    project(s - 8, no)
                else:
                    pe.wait_ge(x1_ready, 2 * b)
                    turn(res, s - 12, no)

            def phase_a(b, par, first, last):
                for s in range(STEPS):
                    scores(b, par, s)
                    if s in STACK_STEP and not last:
                        for g in STACK_STEP[s]:
                            stack_transpose(b + 1, g)
                    if s in LATE_STACK and not first:
                        for g in LATE_STACK[s]:
                            stack_transpose(b, g)
                    if s in QKV_STEP and not last:
                        qkv(b + 1, QKV_STEP[s])
                    if s >= 3:
                        weigh_behind(b, par, s - 3)
                    elif not first:
                        weigh_behind(b - 1, 1 - par, s - 3 + STEPS)
                    if s >= 2:
                        prob_transpose(b, s - 2)
                    elif not first:
                        prob_transpose(b - 1, s - 2 + STEPS)
                    shared(b, s, first, False)

            pe.wait_ge(wattn_split, 2)
            pe.wait_ge(const_set, 7)
            for t in range(NT):
                qkv(0, t)
                for part in range(NST):
                    stack_transpose(0, NST * t + part)
            over_blocks(pe, phase_a)
            for s in range(14):
                if s < 3:
                    weigh_behind(NB - 1, 1, s - 3 + STEPS)
                if s < 2:
                    prob_transpose(NB - 1, s - 2 + STEPS)
                shared(NB, s, False, True)

            pe.wait_ge(shared_read, shared_uses(NB, 13, False, True) + 1)

            def split_products(acc, w_hi, w_lo, a_hi, a_lo, start, stop):
                pe.matmul(acc, w_hi, a_hi, start=start, stop=False)
                pe.matmul(acc, w_hi, a_lo, start=False, stop=False)
                return pe.matmul(acc, w_lo, a_hi, start=False, stop=stop)

            def phase_b(b, first):
                pe.wait_ge(bx_ready, b + 1)
                for m in range(KH):
                    if first:
                        pe.wait_ge(wb_in[m], 32)
                    for u, (acc, done) in enumerate(((ps_gate, gate_done), (ps_up, up_done))):
                        wait_count(pe, (silu_ready, h0_ready)[u], KH * b + m - 1)
                        for kc in range(KD):
                            at = (u * KD + kc) * P
                            mm = split_products(acc[m % 2][:, :], wglu_hi[:, m, at:at + P], wglu_lo[:, m, at:at + P],
                                                bx_hi[:, kc, :], bx_lo[:, kc, :], kc == 0, kc == KD - 1)
                        mm.then_inc(done, 1)
                for m in range(KH):
                    if first:
                        pe.wait_ge(wh1_in[m], 32)
                    wait_count(pe, h1_ready, KH * b + m - 1)
                    for k in range(KH):
                        if m == 0:
                            pe.wait_ge(h0_split, KH * b + k + 1)
                        mm = split_products(ps_h[m % 2][:, :], wh1_hi[:, m, k * P:(k + 1) * P],
                                            wh1_lo[:, m, k * P:(k + 1) * P], h0_hi[:, k, :], h0_lo[:, k, :],
                                            k == 0, k == KH - 1)
                    mm.then_inc(h1_mm, 1)

            phase_b(0, True)
            with pe.Fori(1, NB) as b:
                phase_b(b, False)

            pe.wait_ge(h1_ready, KH * NB)
            pe.wait_ge(h0_ready, KH * NB)

            def third(b, m):
                pe.wait_ge(h2_split, KH * b + m + 1)
                if m == 0:
                    wait_count(pe, oT_ready, KD * b)
                for kc in range(KD):
                    mm = split_products(ps_oT[kc][:, :], w3_hi[:, m, kc * P:(kc + 1) * P],
                                        w3_lo[:, m, kc * P:(kc + 1) * P], h2_hi[m % 2][:, :], h2_lo[m % 2][:, :],
                                        m == 0, m == KH - 1)
                mm.then_inc(w3_done, 1)

            def to_rows(b):
                pe.wait_ge(oT_ready, KD * (b + 1))
                for pair in range(2):
                    wait_count(pe, y_sum, 2 * b + pair)
                    for u in range(2):
                        t = 2 * pair + u
                        for kc in range(KD):
                            mm = pe.transpose(ps_y[pair][:, u * D + kc * P:u * D + (kc + 1) * P],
                                              oT_s[:, kc, t * P:(t + 1) * P], ident_s[:, :])
                    mm.then_inc(yT_done, 1)

            def phase_c(b, par, first, last):
                for m in range(KH):
                    if first:
                        pe.wait_ge(wh2_in[m], 32)
                    wait_count(pe, h2_ready, KH * b + m - 1)
                    for k in range(KH):
                        if m == 0:
                            pe.wait_ge(h1_split, KH * b + k + 1)
                        mm = split_products(ps_h[m % 2][:, :], wh2_hi[:, m, k * P:(k + 1) * P],
                                            wh2_lo[:, m, k * P:(k + 1) * P], h1_hi[par][:, k, :],
                                            h1_lo[par][:, k, :], k == 0, k == KH - 1)
                    mm.then_inc(h2_mm, 1)
                    if first and m == 1:
                        pe.wait_ge(w3_in, 16 * 2 * KH)
                    if m >= 1:
                        third(b, m - 1)
                    elif not first:
                        third(b - 1, KH - 1)
                    if m == 1 and not first:
                        to_rows(b - 1)

            over_blocks(pe, phase_c)
            third(NB - 1, KH - 1)
            to_rows(NB - 1)

        @block.scalar
        def _(act):
            def split_x(b):
                act.wait_ge(xT_in, 16 * (b + 1))
                wait_count(act, qkv_done, NT * b)
                act.activation(xT_hi[:], xT_s[:], ACT.Copy).then_inc(xT_hi_ready, 1)

            def stage_v(b, par, t):
                act.wait_ge(qkv_done, NT * b + t + 1)
                wait_count(act, head_done, STEPS * (b - 1))
                act.activation(v_s[par][:, t, :, 0:HD], ps_v[:, 0:D].rearrange("p (h d) -> p h d", d=HD),
                               ACT.Copy).then_inc(v_read, 1)

            def stage_hi(b, t):
                act.wait_ge(rope_sum, NT * b + t + 1)
                wait_count(act, stackT_done, NST * (NT * b + t - 1))
                st = stack[t % 2]
                src = qk_s[t % 2][:].rearrange("p (h d) -> p h d", d=HD)
                act.activation(st[:, :, 0, :], src, ACT.Copy).then_inc(stack_hi, 1)
                act.activation(st[:, 0:H, 1, :], src[:, 0:H, :], ACT.Copy).then_inc(stack_hi2, 1)
                act.activation(st[:, H:2 * H, 2, :], src[:, H:2 * H, :], ACT.Copy).then_inc(stack_hi2, 1)

            def stack_out(b, par, g):
                t, part = g // NST, g % NST
                dst = (qT, kT)[part % 2][par]
                act.wait_ge(stackT_done, NST * NT * b + g + 1)
                if g == 0:
                    wait_count(act, score_done, 2 * STEPS * (b - 1))
                act.activation(dst[:, 4 * (part // 2):4 * (part // 2) + 4, t * P:(t + 1) * P],
                               ps_stack[:, :].rearrange("p (j n) -> p j n", n=P), ACT.Copy).then_inc(stackT_read, 1)

            def copy_scores(b, s):
                for r in range(2):
                    act.wait_ge(score_done, 2 * (STEPS * b + s) + r + 1)
                    wait_count(act, exp_done, STEPS * b + s - 1)
                    act.activation(merged_s[s % 2][:, r::2, :],
                                   ps_score[r][:, :].rearrange("p (h n) -> p h n", h=2)[:, :, P:2 * P],
                                   ACT.Copy).then_inc(copied, 1)

            def exponentials(b, s):
                act.wait_ge(low_ready, STEPS * b + s + 1)
                wait_count(act, probT_done, STEPS * b + s - 1)
                for c in range(GH):
                    a = act.activation(prob[s % 2][:, c, :], merged_s[s % 2][:, c, :], ACT.Exp,
                                       bias=low[s % 2][:, c:c + 1], scale=-1.0)
                a.then_inc(exp_done, 1)

            def head_out(b, hg, turned):
                act.wait_ge(head_done, STEPS * b + NT * hg + NT)
                wait_count(act, shared_done, turned)
                act.activation(headT[:, :], ps_head[:, :], ACT.Copy).then_inc(head_read, 1)

            def shared(b, s, first, flush):
                if first or s not in (4, 5, 12, 13):
                    return
                act.wait_ge(shared_done, shared_uses(b, s, first, flush) + 1)
                if s in (4, 5):
                    act.activation(attT_hi[:, s - 4, :], ps_shared[:, :], ACT.Copy).then_inc(shared_hi, 1)
                else:
                    if s == 12:
                        act.wait_ge(x1T_out, 16 * b)
                    act.activation(x1T_s[:, s - 12, :], ps_shared[:, :], ACT.Copy).then_inc(shared_read, 1)

            def phase_a(b, par, first, last):
                for s in range(STEPS):
                    if s % NT:
                        copy_scores(b, s)
                    if s == 0 and not last:
                        split_x(b + 1)
                    if s in STACK_STEP and not last:
                        for g in STACK_STEP[s]:
                            stack_out(b + 1, 1 - par, g)
                    if s in LATE_STACK and not first:
                        for g in LATE_STACK[s]:
                            stack_out(b, par, g)
                    if s - 1 in QKV_STEP and not last:
                        stage_v(b + 1, 1 - par, QKV_STEP[s - 1])
                        stage_hi(b + 1, QKV_STEP[s - 1])
                    if s % NT == 2:
                        if s >= 6:
                            head_out(b, s // NT - 1, 0 if first and s == 6 else shared_uses(b, s - 3, first, False) + 1)
                        elif not first:
                            head_out(b - 1, NG - 1, shared_uses(b - 1, 15, False, False) + 1)
                    shared(b, s, first, False)
                    exponentials(b, s)

            split_x(0)
            act.wait_ge(wattn_in, 32)
            act.activation(wq_hi[:], wq_f[:], ACT.Copy).then_inc(wattn_hi, 1)
            act.activation(wo_hi[:], wo_f[:], ACT.Copy).then_inc(wattn_hi, 1)
            for t in range(NT):
                stage_v(0, 0, t)
                stage_hi(0, t)
                for part in range(NST):
                    stack_out(0, 0, NST * t + part)
            over_blocks(act, phase_a)
            for s in range(14):
                if s == 2:
                    head_out(NB - 1, NG - 1, shared_uses(NB - 1, 15, False, False) + 1)
                shared(NB, s, False, True)

            def split_bx(b):
                act.wait_ge(bx_in, 16 * (b + 1))
                wait_count(act, up_done, KH * b)
                act.activation(bx_hi[:], bx_s[:], ACT.Copy).then_inc(bx_hi_ready, 1)

            def h0_high(b, m):
                act.wait_ge(h0_ready, KH * b + m + 1)
                wait_count(act, h1_mm, KH * b)
                act.activation(h0_hi[:, m, :], h0_s[m % 2][:], ACT.Copy).then_inc(h0_hi_ready, 1)

            def phase_b(b, last):
                for m in range(KH):
                    act.wait_ge(gate_done, KH * b + m + 1)
                    wait_count(act, h0_ready, KH * b + m - 1)
                    act.activation(silu_s[m % 2][:], ps_gate[m % 2][:, :], ACT.Silu,
                                   scale=s1_s[:, m:m + 1]).then_inc(silu_ready, 1)
                    if m:
                        h0_high(b, m - 1)
                h0_high(b, KH - 1)
                for m in range(KH):
                    act.wait_ge(h1_mm, KH * b + m + 1)
                    wait_count(act, h1_out[m % 2], 16 * (KH // 2 * b + m // 2))
                    act.activation(h1_s[m % 2][:], ps_h[m % 2][:, :], ACT.Gelu,
                                   scale=sh1_s[:, m:m + 1]).then_inc(h1_ready, 1)
                    if m == 1 and not last:
                        split_bx(b + 1)

            split_bx(0)
            phase_b(0, False)
            with act.Fori(1, NB - 1) as b:
                phase_b(b, False)
            phase_b(NB - 1, True)

            def split_h1(b, par, k):
                act.wait_ge(h1_in_s[k % 4], 16 * (KH // 4 * b + k // 4 + 1))
                wait_count(act, h2_mm, KH * (b - 1))
                act.activation(h1_hi[par][:, k, :], h1_in[k % 4][:], ACT.Copy).then_inc(h1_hi_ready, 1)

            def out_features(b):
                act.wait_ge(w3_done, KH * (b + 1))
                for kc in range(KD):
                    act.activation(oT_s[:, kc, :], ps_oT[kc][:, :], ACT.Copy,
                                   scale=s3_s[:, kc:kc + 1]).then_inc(oT_ready, 1)

            def phase_c(b, par, first, last):
                for m in range(KH):
                    act.wait_ge(h2_mm, KH * b + m + 1)
                    wait_count(act, h2_split, KH * b + m - 1)
                    act.activation(h2_s[m % 2][:], ps_h[m % 2][:, :], ACT.Gelu,
                                   scale=sh2_s[:, m:m + 1]).then_inc(h2_ready, 1)
                    act.wait_ge(h2_ready, KH * b + m + 1)
                    wait_count(act, w3_done, KH * b + m - 1)
                    act.activation(h2_hi[m % 2][:], h2_s[m % 2][:], ACT.Copy).then_inc(h2_hi_ready, 1)
                    if m == 0 and not first:
                        out_features(b - 1)
                    if not last:
                        split_h1(b + 1, 1 - par, m)

            for k in range(KH):
                split_h1(0, 0, k)
            over_blocks(act, phase_c)
            out_features(NB - 1)

        @block.vector
        def _(dve):
            dve.memset(neg_half[:], -0.5).then_inc(const_set, 1)
            for st in stack:
                dve.memset(st[:, :, 3, :].bitcast(F32), 0.0).then_inc(const_set, 1)
            for v in v_s:
                dve.memset(v[:, :, :, HD:2 * HD], 1.0).then_inc(const_set, 1)
            dve.wait_ge(const_in, 16 * N_CONST)
            dve.tensor_copy(ident_r[:], ident_s[:]).then_inc(const_set, 1)
            dve.tensor_scalar(take_s[:], bias_s[:], 1.0, None, ALU.is_gt).then_inc(const_set, 1)
            dve.wait_ge(const_set, 7)

            def split_x(b):
                dve.wait_ge(xT_hi_ready, b + 1)
                dve.tensor_tensor(xT_lo[:], xT_s[:], xT_hi[:].bitcast(F32), ALU.subtract).then_inc(xT_ready, 1)

            def rope(b, t):
                dve.wait_ge(qkv_done, NT * b + t + 1)
                wait_count(dve, rope_sum, NT * b + t)
                x4 = ps_qk[:, :].rearrange("p (q h d) -> p q h d", q=2, d=HD)
                b4 = rope_b[:].rearrange("p (q h d) -> p q h d", q=2, d=HD)
                a3 = rope_a[:].rearrange("p (q g e) -> p q g e", q=2, e=HALF)
                x3 = ps_qk[:, :].rearrange("p (q g e) -> p q g e", q=2, e=HALF)
                dve.tensor_tensor(a3, x3, cos_s[:, t].unsqueeze(2).broadcast_to([P, 2, 2 * H, HALF]),
                                  ALU.mult).then_inc(rope_terms, 1)
                dve.tensor_tensor(b4[:, :, :, 0:HALF], x4[:, :, :, HALF:HD],
                                  nsin_s[:, t].unsqueeze(2).broadcast_to([P, 2, H, HALF]),
                                  ALU.mult).then_inc(rope_terms, 1)
                dve.tensor_tensor(b4[:, :, :, HALF:HD], x4[:, :, :, 0:HALF],
                                  sin_s[:, t].unsqueeze(2).broadcast_to([P, 2, H, HALF]),
                                  ALU.mult).then_inc(qk_read, 1)
                dve.wait_ge(rope_terms, 2 * (NT * b + t + 1))
                dve.wait_ge(qk_read, NT * b + t + 1)
                wait_count(dve, stack_hi2, 2 * (NT * b + t - 1))
                wait_count(dve, stack_lo, 2 * (NT * b + t - 1))
                dve.tensor_tensor(qk_s[t % 2][:], rope_a[:], rope_b[:], ALU.add).then_inc(rope_sum, 1)

            def merge(b, s):
                for r in range(2):
                    dst = merged_s[s % 2][:, r::2, :]
                    src = ps_score[r][:, :].rearrange("p (h n) -> p h n", h=2)[:, :, 0:P]
                    if s % NT == 0:
                        dve.wait_ge(score_done, 2 * (STEPS * b + s) + r + 1)
                        wait_count(dve, exp_done, STEPS * b + s - 1)
                        dve.tensor_tensor(dst, src, bias_s[:].unsqueeze(1).broadcast_to([P, 2, P]),
                                          ALU.add).then_inc(merged, 1)
                    else:
                        dve.wait_ge(copied, 2 * (NT - 1) * (NG * b + s // NT) + 2 * (s % NT - 1) + r + 1)
                        dve.nop(nofuse=True)
                        dve.copy_predicated(dst, take_s[:].unsqueeze(1).broadcast_to([P, 2, P]),
                                            src).then_inc(merged, 1)
                dve.wait_ge(merged, 2 * (STEPS * b + s) + 2)
                wait_count(dve, exp_done, STEPS * b + s - 1)
                dve.tensor_reduce(low[s % 2][:], merged_s[s % 2][:], AX.X, ALU.min).then_inc(low_ready, 1)

            def probs_out(b, s):
                i = s % NT
                src = ps_probT[:, :].rearrange("p (c n) -> p c n", n=P)
                dve.wait_ge(probT_done, STEPS * b + s + 1)
                wait_count(dve, head_done, STEPS * b + s - 1)
                op = dve.tensor_tensor(probT[i % 2][:, :, 0:P], src,
                                       lower_s[:].unsqueeze(1).broadcast_to([P, GH, P]), ALU.mult)
                if i:
                    op = dve.tensor_tensor(probT[(i - 1) % 2][:, :, P:2 * P], src,
                                           upper_s[:].unsqueeze(1).broadcast_to([P, GH, P]), ALU.mult)
                op.then_inc(probT_read, 1)

            def normalise(b, hg, no):
                dve.wait_ge(shared_done, no + 1)
                sums = ps_shared[:, :].rearrange("p (t c e) -> p t c e", c=GH, e=2 * HD)
                dve.reciprocal(denom[:], sums[:, :, :, HD]).then_inc(denom_ready, 1)
                dve.wait_ge(denom_ready, NG * b + hg + 1)
                dst = att[:].rearrange("p t (g c d) -> p t g c d", g=NG, d=HD)[:, :, hg]
                dve.tensor_tensor(dst, sums[:, :, :, 0:HD], denom[:].unsqueeze(3).broadcast_to([P, NT, GH, HD]),
                                  ALU.mult).then_inc(shared_read, 1)

            def residual(b, par, pair, no):
                dve.wait_ge(shared_done, no + 1)
                if pair == 0:
                    dve.wait_ge(x_in, 16 * (b + 1))
                    dve.wait_ge(x1_out, 16 * (b + 1))
                r = res[:, 2 * pair:2 * pair + 2, :]
                dve.tensor_tensor(r, ps_shared[:, :].rearrange("p (t d) -> p t d", t=2),
                                  x_s[par][:, 2 * pair:2 * pair + 2, :], ALU.add).then_inc(shared_read, 1)
                dve.wait_ge(shared_read, no + 1)
                statistics(res, pair, b, stats_ready, mean_ready)

            def statistics(src, pair, b, stats_sem, mean_sem):
                for u in range(2):
                    dve.bn_stats(stats[:, 2 * pair + u, :], src[:, 2 * pair + u, :]).then_inc(stats_sem, 1)
                dve.wait_ge(stats_sem, 2 * (2 * b + pair) + 2)
                dve.nop(nofuse=True)
                for u in range(2):
                    dve.bn_aggr(meanvar[:, 2 * pair + u, :], stats[:, 2 * pair + u, :]).then_inc(mean_sem, 1)

            def normed(src, dst, pair, b, rstd_sem, ready):
                dve.wait_ge(rstd_sem, 2 * b + pair + 1)
                for u in range(2):
                    t = 2 * pair + u
                    op = dve.tensor_scalar(dst[:, t, :], src[:, t, :], meanvar[:, t, 0:1], rstd[:, t:t + 1],
                                           ALU.subtract, ALU.mult)
                op.then_inc(ready, 1)

            def shared(b, par, s, first, flush):
                if s not in SHARED_STEPS or (first and s not in (7, 11, 15)) or (flush and s not in LAST_SHARED_STEPS):
                    return
                no = shared_uses(b, s, first, flush)
                if s == 3:
                    normalise(b - 1, NG - 1, no)
                elif s % 4 == 3:
                    normalise(b, s // 4 - 1, no)
                elif s in (4, 5):
                    dve.wait_ge(shared_hi, KD * (b - 1) + s - 3)
                    dve.tensor_tensor(attT_lo[:, s - 4, :], ps_shared[:, :], attT_hi[:, s - 4, :].bitcast(F32),
                                      ALU.subtract).then_inc(shared_read, 1)
                elif s in (8, 9):
                    residual(b - 1, 1 - par, s - 8, no)

            def phase_a(b, par, first, last):
                for s in range(STEPS):
                    merge(b, s)
                    if s == 0 and not last:
                        split_x(b + 1)
                    if s >= 2:
                        probs_out(b, s - 2)
                    elif not first:
                        probs_out(b - 1, s - 2 + STEPS)
                    if s in (10, 11) and not first:
                        normed(res, res, s - 10, b - 1, rstd_ready, x1_ready)
                    if s in QKV_STEP and not last:
                        rope(b + 1, QKV_STEP[s])
                    shared(b, par, s, first, False)

            split_x(0)
            dve.wait_ge(wattn_hi, 2)
            dve.tensor_tensor(wq_lo[:], wq_f[:], wq_hi[:].bitcast(F32), ALU.subtract).then_inc(wattn_split, 1)
            dve.tensor_tensor(wo_lo[:], wo_f[:], wo_hi[:].bitcast(F32), ALU.subtract).then_inc(wattn_split, 1)
            for t in range(NT):
                rope(0, t)
            over_blocks(dve, phase_a)
            for s in range(14):
                if s < 2:
                    probs_out(NB - 1, s - 2 + STEPS)
                if s in (10, 11):
                    normed(res, res, s - 10, NB - 1, rstd_ready, x1_ready)
                shared(NB, 0, s, False, True)

            def split_bx(b):
                dve.wait_ge(bx_hi_ready, b + 1)
                dve.tensor_tensor(bx_lo[:], bx_s[:], bx_hi[:].bitcast(F32), ALU.subtract).then_inc(bx_ready, 1)

            def h0_low(b, m):
                dve.wait_ge(h0_hi_ready, KH * b + m + 1)
                dve.tensor_tensor(h0_lo[:, m, :], h0_s[m % 2][:], h0_hi[:, m, :].bitcast(F32),
                                  ALU.subtract).then_inc(h0_split, 1)

            def phase_b(b, last):
                for m in range(KH):
                    dve.wait_ge(up_done, KH * b + m + 1)
                    dve.wait_ge(silu_ready, KH * b + m + 1)
                    wait_count(dve, h0_split, KH * b + m - 1)
                    dve.scalar_tensor_tensor(h0_s[m % 2][:], ps_up[m % 2][:, :], s2_s[:, m:m + 1],
                                             silu_s[m % 2][:], ALU.mult, ALU.mult).then_inc(h0_ready, 1)
                    if m:
                        h0_low(b, m - 1)
                h0_low(b, KH - 1)
                if not last:
                    split_bx(b + 1)

            split_bx(0)
            phase_b(0, False)
            with dve.Fori(1, NB - 1) as b:
                phase_b(b, False)
            phase_b(NB - 1, True)

            def split_h1(b, par, k):
                dve.wait_ge(h1_hi_ready, KH * b + k + 1)
                dve.tensor_tensor(h1_lo[par][:, k, :], h1_in[k % 4][:], h1_hi[par][:, k, :].bitcast(F32),
                                  ALU.subtract).then_inc(h1_split, 1)

            def out_rows(b, pair):
                dve.wait_ge(yT_done, 2 * b + pair + 1)
                if pair == 0:
                    dve.wait_ge(x1_in, 16 * (b + 1))
                    dve.wait_ge(y_out, 16 * (b + 1))
                dve.tensor_tensor(y_s[:, 2 * pair:2 * pair + 2, :], ps_y[pair][:, :].rearrange("p (t d) -> p t d", t=2),
                                  x1_s[:, 2 * pair:2 * pair + 2, :], ALU.add).then_inc(y_sum, 1)
                dve.wait_ge(y_sum, 2 * b + pair + 1)
                statistics(y_s, pair, b, cstats_ready, cmean_ready)

            def phase_c(b, par, first, last):
                for m in range(KH):
                    dve.wait_ge(h2_hi_ready, KH * b + m + 1)
                    dve.tensor_tensor(h2_lo[m % 2][:], h2_s[m % 2][:], h2_hi[m % 2][:].bitcast(F32),
                                      ALU.subtract).then_inc(h2_split, 1)
                    if not last:
                        split_h1(b + 1, 1 - par, m)
                    if not first and m in (1, 2):
                        out_rows(b - 1, m - 1)
                    if not first and m in (3, 4):
                        normed(y_s, y_s, m - 3, b - 1, crstd_ready, y_ready)

            for k in range(KH):
                split_h1(0, 0, k)
            over_blocks(dve, phase_c)
            for pair in range(2):
                out_rows(NB - 1, pair)
            for pair in range(2):
                normed(y_s, y_s, pair, NB - 1, crstd_ready, y_ready)

        @block.gpsimd
        def _(pool):
            def stack_low(b, t):
                st = stack[t % 2]
                src = qk_s[t % 2][:].rearrange("p (h d) -> p h d", d=HD)
                pool.wait_ge(stack_hi, NT * b + t + 1)
                pool.tensor_tensor(st[:, 0:H, 2, :], src[:, 0:H, :], st[:, 0:H, 0, :].bitcast(F32),
                                   ALU.subtract).then_inc(stack_lo, 1)
                pool.tensor_tensor(st[:, H:2 * H, 1, :], src[:, H:2 * H, :], st[:, H:2 * H, 0, :].bitcast(F32),
                                   ALU.subtract).then_inc(stack_lo, 1)

            def split_piece(b, q):
                pool.wait_ge(piece_in, 16 * (NPIECE * b + q + 1))
                wait_count(pool, piece_out, 32 * (NPIECE * b + q))
                pool.nop(nofuse=True)
                pool.tensor_scalar(piece_hi[:], piece[:], 1.0, 1.0, ALU.mult, ALU.mult).then_inc(piece_hi_ready, 1)
                pool.wait_ge(piece_hi_ready, NPIECE * b + q + 1)
                pool.tensor_tensor(piece_lo[:], piece[:], piece_hi[:].bitcast(F32),
                                   ALU.subtract).then_inc(piece_lo_ready, 1)

            def inverse_deviation(b, pair, mean_sem, step, ready):
                n = 5 * (2 * b + pair)
                ab = slice(2 * pair, 2 * pair + 2)
                v, y, t, r = vareps[:, ab], rstd0[:, ab], rsq[:, ab], rstd[:, ab]
                pool.wait_ge(mean_sem, 2 * (2 * b + pair) + 2)
                pool.nop(nofuse=True)
                pool.tensor_scalar(v, meanvar[:, ab, 1], EPS, None, ALU.add).then_inc(step, 1)
                pool.wait_ge(step, n + 1)
                pool.tensor_tensor(y, v, neg_half[:, ab], ALU.pow).then_inc(step, 1)
                pool.wait_ge(step, n + 2)
                pool.tensor_tensor(t, y, y, ALU.mult).then_inc(step, 1)
                pool.wait_ge(step, n + 3)
                pool.tensor_tensor(t, t, v, ALU.mult).then_inc(step, 1)
                pool.wait_ge(step, n + 4)
                pool.nop(nofuse=True)
                pool.tensor_scalar(t, t, -0.5, 1.5, ALU.mult, ALU.add).then_inc(step, 1)
                pool.wait_ge(step, n + 5)
                pool.tensor_tensor(r, y, t, ALU.mult).then_inc(ready, 1)

            def phase_a(b, par, first, last):
                split_piece(b, 0)
                if not last:
                    stack_low(b + 1, 0)
                    stack_low(b + 1, 1)
                split_piece(b, 1)
                if not last:
                    stack_low(b + 1, 2)
                if not first:
                    inverse_deviation(b - 1, 0, mean_ready, rstd_step, rstd_ready)
                    inverse_deviation(b - 1, 1, mean_ready, rstd_step, rstd_ready)
                split_piece(b, 2)
                if not last:
                    stack_low(b + 1, 3)
                split_piece(b, 3)

            for t in range(NT):
                stack_low(0, t)
            over_blocks(pool, phase_a)
            for pair in range(2):
                inverse_deviation(NB - 1, pair, mean_ready, rstd_step, rstd_ready)
            with pool.Fori(0, NB) as b:
                for pair in range(2):
                    inverse_deviation(b, pair, cmean_ready, crstd_step, crstd_ready)


def constants():
    theta = (1.0 / 10000.0 ** (np.arange(HALF, dtype=np.float32) / HALF)).astype(np.float32)
    freqs = np.arange(TB, dtype=np.float32)[:, None] * theta[None, :]
    by_tile = lambda a: np.ascontiguousarray(a.reshape(NT, P, HALF).transpose(1, 0, 2))
    scale = np.array([-1.0 / np.sqrt(HD), 1.0], np.float32)[None, None, :, None]
    cos = by_tile(np.cos(freqs).astype(np.float32))[:, :, None, :] * scale
    sin = by_tile(np.sin(freqs).astype(np.float32))[:, :, None, :] * scale
    row, col = np.arange(P)[:, None], np.arange(P)[None, :]
    return {
        "cos": cos,
        "sin": np.stack([sin, -sin]),
        "lower": (row <= col).astype(np.float32),
        "upper": (row > col).astype(np.float32),
        "bias": np.where(col > row, np.float32(MASKED), np.float32(0)),
        "ident": np.eye(P, dtype=np.float32),
    }


def kernel(**inputs):
    import concourse.bacc as bacc
    from concourse.bass_utils import run_bass_kernel_spmd

    a = {k.removeprefix("L0_"): np.asarray(v) for k, v in inputs.items()}
    flat = a["attn_x"].reshape(NB * TB, D)

    def chunks(w, k):
        return w.reshape(-1, P, k, P).transpose(0, 3, 2, 1)

    packed = np.concatenate(
        [chunks(a["ffn_w1_w"], KD).reshape(KH, P, -1), chunks(a["ffn_w2_w"], KD).reshape(KH, P, -1),
         chunks(a["ffn_h1_w"], KH).reshape(KH, P, -1), chunks(a["ffn_h2_w"], KH).reshape(KH, P, -1),
         a["ffn_w3_w"].T.reshape(KH, P, D)], axis=2)
    by_chunk = lambda s: s.reshape(-1, P).T
    arrays = {
        "x": flat,
        "xT": flat.reshape(NB, TB, KD, P).transpose(0, 3, 2, 1),
        "wqkv": a["attn_Wqkv"].reshape(KD, P, 3 * D).transpose(1, 0, 2),
        "wout": a["attn_Wout"].reshape(KD, P, D).transpose(1, 0, 2),
        "wffn": packed,
        "s1": by_chunk(a["ffn_w1_s"]), "s2": by_chunk(a["ffn_w2_s"]),
        "sh1": by_chunk(a["ffn_h1_s"]), "sh2": by_chunk(a["ffn_h2_s"]), "s3": by_chunk(a["ffn_w3_s"]),
    } | constants()
    nc = bacc.Bacc("TRN2", target_bir_lowering=False, num_devices=1)
    feed, args = {}, {}
    for name, array in arrays.items():
        array = np.ascontiguousarray(array)
        feed[f"in_{name}"] = array
        args[name] = nc.dram_tensor(f"in_{name}", array.shape, mybir.dt.from_np(array.dtype), kind="ExternalInput").ap()
    out = nc.dram_tensor("out_0", (NB * TB, D), F32, kind="ExternalOutput").ap()
    build(nc, out=out, **args)
    r = run_bass_kernel_spmd(nc, [feed], core_ids=[0])
    return r.results[0]["out_0"].reshape(NB, TB, D)
```

```python
from contextlib import ExitStack

import numpy as np

import concourse.bass as bass
from concourse import mybir

ALU = mybir.AluOpType
ACT = mybir.ActivationFunctionType
AX = mybir.AxisListType
F32 = mybir.dt.float32
F32R = mybir.dt.float32r
U8 = mybir.dt.uint8

P = 128
NB = 8
TB = 512
NT = TB // P
D = 256
KD = D // P
H = 16
HD = D // H
HALF = HD // 2
HID = 1024
KH = HID // P
WINDOW = 128
EPS = 1e-5

GH = 4
NG = H // GH
STEPS = NG * NT
SLOT = 64
PARTS = 3 * HD
NST = 4
MASKED = 3e38
GLU_COLS = 2 * KD * P
HID_COLS = KH * P
W3_COLS = D
PACK = GLU_COLS + 2 * HID_COLS + W3_COLS
NPIECE = 4
PIECE = PACK // NPIECE

QKV_STEP = {2: 0, 6: 1, 9: 2, 13: 3}
STACK_ORDER = [(0, 0), (0, 1), (0, 2), (0, 3), (1, 0), (1, 1), (1, 2), (1, 3),
               (2, 0), (2, 1), (3, 0), (3, 1), (2, 2), (2, 3), (3, 2), (3, 3)]
STACKS_BEFORE_SCORES = (2, 6, 10, 12)
STACKS_OF_TILE = (4, 8, 14, 16)
STACK_LAG = 6
STACK_STEP = {s: s - STACK_LAG for s in range(STACK_LAG, STEPS)}
LATE_STACK = {s: STEPS - STACK_LAG + s for s in range(STACK_LAG)}
SHARED_STEPS = (0, 4, 5, 6, 8, 9, 10, 12, 14, 15)
FIRST_SHARED_STEPS = (8, 12)
FLUSH_SHARED_STEPS = (0, 4, 5, 6, 9, 10, 14, 15)
FLUSH_STEPS = 16
TO_TOKENS = {0: (-1, 2), 4: (-1, 3), 8: (0, 0), 12: (0, 1)}
PIECE_STEP = {1: 0, 5: 1, 9: 2, 13: 3}


def shared_uses(b, s, first, flush):
    if first:
        return FIRST_SHARED_STEPS.index(s)
    before_block = len(SHARED_STEPS) * (b - 1) + len(FIRST_SHARED_STEPS)
    return before_block + (FLUSH_SHARED_STEPS if flush else SHARED_STEPS).index(s)


def uses_shared(s, first, flush):
    return s in (FIRST_SHARED_STEPS if first else FLUSH_SHARED_STEPS if flush else SHARED_STEPS)


def uppers(b, s):
    return (NT - 1) * (NG * b + s // NT) + s % NT


def wait_count(eng, sem, count):
    if not isinstance(count, int) or count > 0:
        eng.wait_ge(sem, count)


def over_blocks(eng, block, peeled=1):
    block(0, 0, True, False)
    with eng.Fori(0, (NB - 1 - peeled) // 2) as pair:
        for j in (1, 2):
            block(pair * 2 + j, j % 2, False, False)
    for b in range(NB - peeled, NB):
        block(b, b % 2, False, b == NB - 1)


def build(nc, x, xT, wqkv, wout, wffn, s1, s2, sh1, sh2, s3, cos, sin, lower, upper, bias, ident, out):
    x_v = x.rearrange("(b t p) d -> b p t d", b=NB, t=NT)
    out_v = out.rearrange("(b t p) d -> b p t d", b=NB, t=NT)
    with ExitStack() as ctx:
        def scratch(name, shape, dt=F32):
            return nc.dram_tensor(name, shape, dt, kind="Internal").ap()

        w_hi_d = scratch("w_hi_d", (NB, P, PACK))
        w_lo_d = scratch("w_lo_d", (NB, P, PACK))
        x1_d = scratch("x1_d", (NB, P, NT, D))
        x1T_d = scratch("x1T_d", (NB, P, KD, TB))
        h1_d = scratch("h1_d", (NB, P, KH, TB))

        base = (nc.sbuf_base + 63) // 64 * 64
        cursor = [base]

        def sb(name, shape, dt=F32):
            size = int(np.prod(shape[1:])) * (1 if dt == U8 else 4)
            at = cursor[0]
            cursor[0] += (size + 31) // 32 * 32
            return nc.alloc_sbuf_tensor_at(name, shape, dt, offset=at)

        def bank(name):
            return ctx.enter_context(nc.psum_tensor(name, [P, 512], F32))

        def sem(name):
            return ctx.enter_context(nc.semaphore(name))

        s1_s, s2_s, sh1_s, sh2_s = (sb(n, [P, KH]) for n in ("s1_s", "s2_s", "sh1_s", "sh2_s"))
        s3_s = sb("s3_s", [P, KD])
        ident_s = sb("ident_s", [P, P])
        neg_half = sb("neg_half", [P, 4])
        stats = sb("stats", [P, 4, 6])
        meanvar = sb("meanvar", [P, 4, 2])
        vareps, rstd0, rsq, rstd = (sb(n, [P, 4]) for n in ("vareps", "rstd0", "rsq", "rstd"))
        phase_base = cursor[0]

        ident_r = sb("ident_r", [P, P], F32R)
        wq_hi, wq_lo = sb("wq_hi", [P, KD, 3 * D], F32R), sb("wq_lo", [P, KD, 3 * D], F32R)
        wo_hi, wo_lo = sb("wo_hi", [P, KD, D], F32R), sb("wo_lo", [P, KD, D], F32R)
        qT = [sb(f"qT{i}", [P, H // 2, TB], F32R) for i in range(2)]
        kT = [sb(f"kT{i}", [P, H // 2, TB], F32R) for i in range(2)]
        v_s = [sb(f"v{i}", [P, NT, H, 2 * HD]) for i in range(2)]
        stack = [sb(f"stack{i}", [P, 2 * H, 4, HD], F32R) for i in range(2)]
        xT_s = sb("xT_s", [P, KD, TB])
        xT_hi, xT_lo = sb("xT_hi", [P, KD, TB], F32R), sb("xT_lo", [P, KD, TB], F32R)
        x_s = [sb(f"x_s{i}", [P, NT, D]) for i in range(2)]
        rope_a, rope_b = sb("rope_a", [P, 2 * D]), sb("rope_b", [P, 2 * D])
        qk_s = [sb(f"qk_s{i}", [P, 2 * D]) for i in range(2)]
        merged_s = [sb(f"merged_s{i}", [P, GH, P]) for i in range(2)]
        low = [sb(f"low{i}", [P, GH]) for i in range(2)]
        prob = [sb(f"prob{i}", [P, GH, P]) for i in range(2)]
        turned = [sb(f"turned{i}", [P, GH, P]) for i in range(2)]
        wq_f = nc.alloc_sbuf_tensor_at("wq_f", [P, KD, 3 * D], F32, offset=cursor[0])
        wo_f = nc.alloc_sbuf_tensor_at("wo_f", [P, KD, D], F32, offset=cursor[0] + 4 * KD * 3 * D)
        probT = [sb(f"probT{j}", [P, GH, 2 * P]) for j in range(NT)]
        headT = sb("headT", [P, TB])
        denom = sb("denom", [P, NT, GH])
        att = sb("att", [P, NT, D])
        attT_hi, attT_lo = sb("attT_hi", [P, KD, TB], F32R), sb("attT_lo", [P, KD, TB], F32R)
        res = sb("res", [P, NT, D])
        x1T_s = sb("x1T_s", [P, KD, TB])
        cos_s, sin_s, nsin_s = (sb(n, [P, NT, 2, HALF]) for n in ("cos_s", "sin_s", "nsin_s"))
        lower_s, upper_s, bias_s = (sb(n, [P, P]) for n in ("lower_s", "upper_s", "bias_s"))
        take_s = sb("take_s", [P, P], U8)
        piece = [sb(f"piece{i}", [P, PIECE]) for i in range(2)]
        piece_hi, piece_lo = sb("piece_hi", [P, PIECE], F32R), sb("piece_lo", [P, PIECE], F32R)
        a_end = cursor[0]

        cursor[0] = phase_base
        wh2_hi = sb("wh2_hi", [P, KH, HID_COLS], F32R)
        bc_base = cursor[0]
        wglu_hi, wglu_lo = sb("wglu_hi", [P, KH, GLU_COLS], F32R), sb("wglu_lo", [P, KH, GLU_COLS], F32R)
        after_glu = cursor[0]
        wh1_hi, wh1_lo = sb("wh1_hi", [P, KH, HID_COLS], F32R), sb("wh1_lo", [P, KH, HID_COLS], F32R)
        after_h1w = cursor[0]
        bx_s = sb("bx_s", [P, KD, TB])
        bx_hi, bx_lo = sb("bx_hi", [P, KD, TB], F32R), sb("bx_lo", [P, KD, TB], F32R)
        after_bx = cursor[0] = max(cursor[0], after_h1w + 2 * 4 * KH * D)
        h0_hi, h0_lo = sb("h0_hi", [P, KH, TB], F32R), sb("h0_lo", [P, KH, TB], F32R)
        silu_s = [sb(f"silu_s{i}", [P, TB]) for i in range(2)]
        h0_s = [sb(f"h0_s{i}", [P, TB]) for i in range(2)]
        h1_s = [sb(f"h1_s{i}", [P, TB]) for i in range(2)]
        b_end = cursor[0]

        cursor[0] = bc_base
        wh2_lo = sb("wh2_lo", [P, KH, HID_COLS], F32R)
        assert cursor[0] <= after_glu
        cursor[0] = after_glu
        h1_hi = [sb(f"h1_hi{i}", [P, KH, TB], F32R) for i in range(2)]
        h1_lo = [sb(f"h1_lo{i}", [P, KH, TB], F32R) for i in range(2)]
        assert cursor[0] <= after_h1w
        cursor[0] = after_h1w
        w3_hi, w3_lo = sb("w3_hi", [P, KH, D], F32R), sb("w3_lo", [P, KH, D], F32R)
        assert cursor[0] <= after_bx
        cursor[0] = after_bx
        h1_in = [sb(f"h1_in{i}", [P, TB]) for i in range(4)]
        h2_s = [sb(f"h2_s{i}", [P, TB]) for i in range(2)]
        h2_hi = [sb(f"h2_hi{i}", [P, TB], F32R) for i in range(2)]
        h2_lo = [sb(f"h2_lo{i}", [P, TB], F32R) for i in range(2)]
        oT_s = sb("oT_s", [P, KD, TB])
        x1_s = sb("x1_s", [P, NT, D])
        y_s = sb("y_s", [P, NT, D])
        c_end = cursor[0]
        for end in (a_end, b_end, c_end):
            assert end <= nc.sbuf_usable_end, (a_end, b_end, c_end, nc.sbuf_usable_end)

        banks = [bank(f"bank{i}") for i in range(8)]
        ps_qk, ps_v, ps_stack = banks[0], banks[1], banks[2]
        ps_score = [banks[3], banks[4]]
        ps_probT, ps_head, ps_shared = banks[5], banks[6], banks[7]
        SETUP_BANKS = (ps_stack, ps_head)
        ps_gate, ps_up, ps_h = [banks[0], banks[1]], [banks[2], banks[3]], [banks[4], banks[5]]
        ps_oT = [banks[2], banks[3]]
        ps_y = [banks[6], banks[7]]

        N_CONST = 12
        const_in = sem("const_in")
        wattn_in = [sem("wq0_in"), sem("wq1_in"), sem("wo_in")]
        const_set = sem("const_set")
        wattn_hi = sem("wattn_hi")
        wattn_split = sem("wattn_split")
        xT_in, xT_hi_ready, xT_ready = sem("xT_in"), sem("xT_hi_ready"), sem("xT_ready")
        x_in = sem("x_in")
        qkv_done, qk_read, v_read = sem("qkv_done"), sem("qk_read"), sem("v_read")
        rope_terms, rope_sum = sem("rope_terms"), sem("rope_sum")
        stack_hi, stack_hi2, stack_lo = sem("stack_hi"), sem("stack_hi2"), sem("stack_lo")
        stackT_done, stackT_read = sem("stackT_done"), sem("stackT_read")
        score_done, copied, merged, low_ready = sem("score_done"), sem("copied"), sem("merged"), sem("low_ready")
        exp_done, probT_done, turned_ready = sem("exp_done"), sem("probT_done"), sem("turned_ready")
        lower_ready, upper_ready = sem("lower_ready"), sem("upper_ready")
        head_done, head_read = sem("head_done"), sem("head_read")
        shared_done, shared_read, shared_hi = sem("shared_done"), sem("shared_read"), sem("shared_hi")
        denom_ready = sem("denom_ready")
        stats_ready, mean_ready, rstd_step, rstd_ready = (
            sem("stats_ready"), sem("mean_ready"), sem("rstd_step"), sem("rstd_ready"))
        x1_ready, x1_out, x1T_out = sem("x1_ready"), sem("x1_out"), sem("x1T_out")
        piece_in = [sem("piece_in0"), sem("piece_in1")]
        piece_hi_ready, piece_lo_ready = sem("piece_hi_ready"), sem("piece_lo_ready")
        piece_out = sem("piece_out")
        wb_in = [sem(f"wglu_in{m}") for m in range(KH)]
        wh1_in = [sem(f"wh1_in{m}") for m in range(KH)]
        bx_in, bx_hi_ready, bx_ready = sem("bx_in"), sem("bx_hi_ready"), sem("bx_ready")
        gate_done, up_done, silu_ready, h0_ready = (
            sem("gate_done"), sem("up_done"), sem("silu_ready"), sem("h0_ready"))
        h0_hi_ready, h0_split, h1_mm, h1_ready = sem("h0_hi_ready"), sem("h0_split"), sem("h1_mm"), sem("h1_ready")
        h1_out = [sem("h1_out0"), sem("h1_out1")]
        wh2_in = [sem(f"wh2_in{m}") for m in range(KH)]
        w3_in = sem("w3_in")
        h1_in_s = [sem(f"h1_in_s{i}") for i in range(4)]
        h1_hi_ready, h1_split = sem("h1_hi_ready"), sem("h1_split")
        h2_mm, h2_ready, h2_hi_ready, h2_split = sem("h2_mm"), sem("h2_ready"), sem("h2_hi_ready"), sem("h2_split")
        w3_done, oT_ready, yT_done, y_sum = sem("w3_done"), sem("oT_ready"), sem("yT_done"), sem("y_sum")
        cstats_ready, cmean_ready, crstd_step, crstd_ready = (
            sem("cstats_ready"), sem("cmean_ready"), sem("crstd_step"), sem("crstd_ready"))
        x1_in, y_ready, y_out = sem("x1_in"), sem("y_ready"), sem("y_out")

        block = ctx.enter_context(nc.Block())

        @block.sync
        def _(sp):
            sp.dma_start(wq_f[:, 0], wqkv[:, 0]).then_inc(wattn_in[0], 16)
            sp.dma_start(xT_s[:], xT[0]).then_inc(xT_in, 16)
            sp.dma_start(wq_f[:, 1], wqkv[:, 1]).then_inc(wattn_in[1], 16)
            sp.dma_start(wo_f[:], wout).then_inc(wattn_in[2], 16)
            for dst, src in ((ident_s, ident), (cos_s, cos), (sin_s, sin[0]), (nsin_s, sin[1]), (lower_s, lower),
                             (upper_s, upper), (bias_s, bias), (s1_s, s1), (s2_s, s2),
                             (sh1_s, sh1), (sh2_s, sh2), (s3_s, s3)):
                sp.dma_start(dst[:], src).then_inc(const_in, 16)

            def results(b, flush):
                sp.wait_ge(x1_ready, 2 * b + 2)
                sp.dma_start(x1_d[b], res[:]).then_inc(x1_out, 16)
                sp.wait_ge(shared_read, shared_uses(b + 1, 15, False, flush) + 1)
                sp.dma_start(x1T_d[b], x1T_s[:]).then_inc(x1T_out, 16)

            def load_xT(b):
                sp.wait_ge(xT_ready, b)
                sp.dma_start(xT_s[:], xT[b]).then_inc(xT_in, 16)

            def store_piece(b, q):
                sp.wait_ge(piece_lo_ready, NPIECE * b + q + 1)
                sp.dma_start(w_hi_d[b, :, q * PIECE:(q + 1) * PIECE], piece_hi[:].bitcast(F32)).then_inc(piece_out, 16)
                sp.dma_start(w_lo_d[b, :, q * PIECE:(q + 1) * PIECE], piece_lo[:].bitcast(F32)).then_inc(piece_out, 16)

            def load_piece(b, q):
                wait_count(sp, piece_lo_ready, NPIECE * b + q - 1)
                sp.dma_start(piece[q % 2][:], wffn[b, :, q * PIECE:(q + 1) * PIECE]).then_inc(piece_in[q % 2], 16)

            def phase_a(b, par, first, last):
                load_piece(b, 0)
                load_piece(b, 1)
                if not isinstance(b, int) or b < NB - 2:
                    load_xT(b + 2)
                wait_count(sp, x_in, 16 * b)
                sp.dma_start(x_s[par][:], x_v[b]).then_inc(x_in, 16)
                for q in range(NPIECE):
                    if q == NPIECE - 1 and not first:
                        results(b - 1, False)
                    store_piece(b, q)
                    if q + 2 < NPIECE:
                        load_piece(b, q + 2)

            sp.sem_inc(x1_out, 16)
            sp.sem_inc(x1T_out, 16)
            sp.sem_inc(y_out, 16)
            load_xT(1)
            over_blocks(sp, phase_a, peeled=3)
            results(NB - 1, True)

            sp.wait_ge(piece_out, 16 * 2 * NPIECE * NB)
            sp.wait_ge(x1T_out, 16 * (NB + 1))
            sp.wait_ge(x1_out, 16 * (NB + 1))
            sp.dma_start(bx_s[:], x1T_d[0]).then_inc(bx_in, 16)
            for m in range(KH):
                sp.dma_start(wglu_hi[:, m, :].bitcast(F32), w_hi_d[m, :, 0:GLU_COLS]).then_inc(wb_in[m], 16)
                sp.dma_start(wglu_lo[:, m, :].bitcast(F32), w_lo_d[m, :, 0:GLU_COLS]).then_inc(wb_in[m], 16)
            for m in range(KH):
                sp.dma_start(wh1_hi[:, m, :].bitcast(F32), w_hi_d[m, :, GLU_COLS:GLU_COLS + HID_COLS]).then_inc(wh1_in[m], 16)
                sp.dma_start(wh1_lo[:, m, :].bitcast(F32), w_lo_d[m, :, GLU_COLS:GLU_COLS + HID_COLS]).then_inc(wh1_in[m], 16)
            C2 = GLU_COLS + HID_COLS
            for m in range(KH):
                sp.dma_start(wh2_hi[:, m, :].bitcast(F32), w_hi_d[m, :, C2:C2 + HID_COLS]).then_inc(wh2_in[m], 16)

            def phase_b(b, load_next):
                if load_next:
                    sp.wait_ge(bx_ready, b + 1)
                    sp.dma_start(bx_s[:], x1T_d[b + 1]).then_inc(bx_in, 16)
                for m in range(KH):
                    sp.wait_ge(h1_ready, KH * b + m + 1)
                    sp.dma_start(h1_d[b, :, m, :], h1_s[m % 2][:]).then_inc(h1_out[m % 2], 16)

            with sp.Fori(0, NB - 1) as b:
                phase_b(b, True)
            sp.wait_ge(up_done, KH * NB)
            for m in range(KH):
                sp.dma_start(wh2_lo[:, m, :].bitcast(F32), w_lo_d[m, :, C2:C2 + HID_COLS]).then_inc(wh2_in[m], 16)
            C3 = C2 + HID_COLS
            for m in range(KH):
                sp.dma_start(w3_hi[:, m, :].bitcast(F32), w_hi_d[m, :, C3:PACK]).then_inc(w3_in, 16)
                sp.dma_start(w3_lo[:, m, :].bitcast(F32), w_lo_d[m, :, C3:PACK]).then_inc(w3_in, 16)
            phase_b(NB - 1, False)

            for i in range(2):
                sp.wait_ge(h1_out[i], 16 * NB * KH // 2)

            def load_h1(b, k):
                wait_count(sp, h1_split, KH * b + k - 3)
                sp.dma_start(h1_in[k % 4][:], h1_d[b, :, k, :]).then_inc(h1_in_s[k % 4], 16)

            def results_c(b):
                sp.wait_ge(y_ready, 2 * (b + 1))
                sp.dma_start(out_v[b], y_s[:]).then_inc(y_out, 16)

            for k in range(KH):
                load_h1(0, k)

            def phase_c(b, par, first, last):
                for k in range(KH):
                    if not last:
                        load_h1(b + 1, k)
                    if k == 5:
                        if not first:
                            results_c(b - 1)
                        wait_count(sp, y_sum, 2 * b)
                        sp.dma_start(x1_s[:], x1_d[b]).then_inc(x1_in, 16)

            over_blocks(sp, phase_c)
            results_c(NB - 1)
            sp.wait_ge(y_out, 16 * (NB + 1))

        @block.tensor
        def _(pe):
            def qkv(b, t, kc):
                if t == 0:
                    pe.wait_ge(xT_ready, b + 1)
                if kc == 0:
                    wait_count(pe, qk_read, NT * b + t)
                    wait_count(pe, v_read, NT * b + t)
                if True:
                    xh = xT_hi[:, kc, t * P:(t + 1) * P]
                    xl = xT_lo[:, kc, t * P:(t + 1) * P]
                    for n, (a, w) in enumerate(((xh, wq_hi), (xh, wq_lo), (xl, wq_hi))):
                        first, last = kc == 0 and n == 0, kc == KD - 1 and n == 2
                        pe.matmul(ps_qk[:, :], a, w[:, kc, 0:2 * D], start=first, stop=last)
                        mm = pe.matmul(ps_v[:, 0:D], a, w[:, kc, 2 * D:3 * D], start=first, stop=last)
                if kc == KD - 1:
                    mm.then_inc(qkv_done, 1)

            def stack_transpose(b, g, in_turn=(ps_stack,)):
                t, part = STACK_ORDER[g]
                wait_count(pe, stackT_read, STEPS * b + g + 1 - len(in_turn))
                dst = in_turn[g % len(in_turn)][:, :].bitcast(F32R)
                pe.wait_ge(stack_lo, 2 * (NT * b + t + 1))
                pe.wait_ge(stack_hi2, 2 * (NT * b + t + 1))
                flat = stack[t % 2][:].rearrange("p h s d -> p (h s d)")
                at = (part % 2) * H * SLOT + (part // 2) * 4 * P
                for j in range(4):
                    mm = pe.transpose(dst[:, j * P:(j + 1) * P], flat[:, at + j * P:at + (j + 1) * P],
                                      ident_r[:, :])
                mm.then_inc(stackT_done, 1)

            def scores(b, par, s):
                hg, i = s // NT, s % NT
                if hg == 0:
                    pe.wait_ge(stackT_read, STEPS * b + STACKS_BEFORE_SCORES[i])
                elif s == 2 * NT:
                    pe.wait_ge(stackT_read, NST * NT * (b + 1))
                k0 = max(i - 1, 0) * P
                for j in range(2):
                    hp = 2 * hg + j
                    for r in range(2):
                        if j == 0:
                            wait_count(pe, merged, 2 * (STEPS * b + s - 1) + r + 1)
                        lo = SLOT * r
                        mm = pe.matmul(ps_score[r][:, j * 2 * P:(j + 1) * 2 * P],
                                       qT[par][lo:lo + PARTS, hp, i * P:(i + 1) * P],
                                       kT[par][lo:lo + PARTS, hp, k0:k0 + 2 * P], start=True, stop=True)
                        if j == 1:
                            mm.then_inc(score_done, 1)

            def prob_transpose(b, s):
                wait_count(pe, turned_ready, STEPS * b + s)
                pe.wait_ge(exp_done, STEPS * b + s + 1)
                for c in range(GH):
                    mm = pe.transpose(ps_probT[:, c * P:(c + 1) * P], prob[s % 2][:, c, :], ident_s[:, :])
                mm.then_inc(probT_done, 1)

            def weigh(b, par, s, j):
                hg = s // NT
                if j == 0:
                    wait_count(pe, head_read, NG * b + hg)
                n = 2 * P if j < NT - 1 else P
                for c in range(GH):
                    mm = pe.matmul(ps_head[32 * c:32 * c + 32, j * P:j * P + n], v_s[par][:, j, hg * GH + c, :],
                                   probT[j][:, c, 0:n], start=(j == 0), stop=(j == NT - 1),
                                   skip_group_check=True)
                mm.then_inc(head_done, 1)

            def weigh_behind(b, par, s):
                i = s % NT
                if i >= 1:
                    pe.wait_ge(lower_ready, STEPS * b + s)
                    pe.wait_ge(upper_ready, uppers(b, s))
                    weigh(b, par, s, i - 1)
                if i == NT - 1:
                    pe.wait_ge(lower_ready, STEPS * b + s + 1)
                    weigh(b, par, s, i)

            def to_tokens(b, hg, no):
                pe.wait_ge(head_read, NG * b + hg + 1)
                wait_count(pe, shared_read, no)
                for t in range(NT):
                    mm = pe.transpose(ps_shared[:, t * P:(t + 1) * P], headT[:, t * P:(t + 1) * P], ident_s[:, :])
                mm.then_inc(shared_done, 1)

            def turn(src, kc, no):
                pe.wait_ge(shared_read, no)
                for t in range(NT):
                    mm = pe.transpose(ps_shared[:, t * P:(t + 1) * P], src[:, t, kc * P:(kc + 1) * P], ident_s[:, :])
                mm.then_inc(shared_done, 1)

            def project(pair, no):
                pe.wait_ge(shared_read, no)
                n = 0
                for u in range(2):
                    t = 2 * pair + u
                    for kc in range(KD):
                        ah, al = (a[:, kc, t * P:(t + 1) * P] for a in (attT_hi, attT_lo))
                        for a, w in ((ah, wo_hi), (ah, wo_lo), (al, wo_hi)):
                            mm = pe.matmul(ps_shared[:, u * D:(u + 1) * D], a, w[:, kc, :], start=(n == 0),
                                           stop=(n % 6 == 5), skip_group_check=True)
                            n += 1
                mm.then_inc(shared_done, 1)

            def shared(b, s, first, flush):
                if not uses_shared(s, first, flush):
                    return
                no = shared_uses(b, s, first, flush)
                if s in TO_TOKENS:
                    back, hg = TO_TOKENS[s]
                    to_tokens(b + back, hg, no)
                elif s in (5, 6):
                    turn(att, s - 5, no)
                elif s in (9, 10):
                    project(s - 9, no)
                else:
                    if s == 14:
                        pe.wait_ge(x1_ready, 2 * b)
                    turn(res, s - 14, no)

            def phase_a(b, par, first, last):
                for s in range(STEPS):
                    scores(b, par, s)
                    if s >= 2:
                        prob_transpose(b, s - 2)
                    elif not first:
                        prob_transpose(b - 1, s - 2 + STEPS)
                    if s in STACK_STEP and not last:
                        stack_transpose(b + 1, STACK_STEP[s])
                    if s in LATE_STACK:
                        stack_transpose(b, LATE_STACK[s])
                    for kc in range(KD):
                        if s + 1 - kc in QKV_STEP and not last:
                            qkv(b + 1, QKV_STEP[s + 1 - kc], kc)
                    if s >= 4:
                        weigh_behind(b, par, s - 4)
                    elif not first:
                        weigh_behind(b - 1, 1 - par, s - 4 + STEPS)
                    shared(b, s, first, False)

            for kc in range(KD):
                pe.wait_ge(wattn_split, kc + 1)
                qkv(0, 0, kc)
            pe.wait_ge(const_set, 7)
            for t in range(1, NT):
                for kc in range(KD):
                    qkv(0, t, kc)
                for g in range(NST * (t - 1), min(NST * t, LATE_STACK[0])):
                    stack_transpose(0, g, SETUP_BANKS)
            pe.wait_ge(wattn_split, 3)
            over_blocks(pe, phase_a)
            for s in range(FLUSH_STEPS):
                if s < 4:
                    weigh_behind(NB - 1, 1, s - 4 + STEPS)
                if s < 2:
                    prob_transpose(NB - 1, s - 2 + STEPS)
                shared(NB, s, False, True)

            pe.wait_ge(shared_read, shared_uses(NB, 15, False, True) + 1)

            def split_products(acc, w_hi, w_lo, a_hi, a_lo, start, stop):
                pe.matmul(acc, w_hi, a_hi, start=start, stop=False)
                pe.matmul(acc, w_hi, a_lo, start=False, stop=False)
                return pe.matmul(acc, w_lo, a_hi, start=False, stop=stop)

            def phase_b(b, first):
                pe.wait_ge(bx_ready, b + 1)
                for m in range(KH):
                    if first:
                        pe.wait_ge(wb_in[m], 32)
                    for u, (acc, done) in enumerate(((ps_gate, gate_done), (ps_up, up_done))):
                        wait_count(pe, (silu_ready, h0_ready)[u], KH * b + m - 1)
                        for kc in range(KD):
                            at = (u * KD + kc) * P
                            mm = split_products(acc[m % 2][:, :], wglu_hi[:, m, at:at + P], wglu_lo[:, m, at:at + P],
                                                bx_hi[:, kc, :], bx_lo[:, kc, :], kc == 0, kc == KD - 1)
                        mm.then_inc(done, 1)
                for m in range(KH):
                    if first:
                        pe.wait_ge(wh1_in[m], 32)
                    wait_count(pe, h1_ready, KH * b + m - 1)
                    for k in range(KH):
                        if m == 0:
                            pe.wait_ge(h0_split, KH * b + k + 1)
                        mm = split_products(ps_h[m % 2][:, :], wh1_hi[:, m, k * P:(k + 1) * P],
                                            wh1_lo[:, m, k * P:(k + 1) * P], h0_hi[:, k, :], h0_lo[:, k, :],
                                            k == 0, k == KH - 1)
                    mm.then_inc(h1_mm, 1)

            phase_b(0, True)
            with pe.Fori(1, NB) as b:
                phase_b(b, False)

            pe.wait_ge(h1_ready, KH * NB)
            pe.wait_ge(h0_ready, KH * NB)

            def third(b, m):
                pe.wait_ge(h2_split, KH * b + m + 1)
                if m == 0:
                    wait_count(pe, oT_ready, KD * b)
                for kc in range(KD):
                    mm = split_products(ps_oT[kc][:, :], w3_hi[:, m, kc * P:(kc + 1) * P],
                                        w3_lo[:, m, kc * P:(kc + 1) * P], h2_hi[m % 2][:, :], h2_lo[m % 2][:, :],
                                        m == 0, m == KH - 1)
                mm.then_inc(w3_done, 1)

            def to_rows(b):
                pe.wait_ge(oT_ready, KD * (b + 1))
                wait_count(pe, y_sum, 2 * b)
                for pair in range(2):
                    for u in range(2):
                        t = 2 * pair + u
                        for kc in range(KD):
                            mm = pe.transpose(ps_y[pair][:, u * D + kc * P:u * D + (kc + 1) * P],
                                              oT_s[:, kc, t * P:(t + 1) * P], ident_s[:, :])
                    mm.then_inc(yT_done, 1)

            def phase_c(b, par, first, last):
                for m in range(KH):
                    if first:
                        pe.wait_ge(wh2_in[m], 32)
                    wait_count(pe, h2_ready, KH * b + m - 1)
                    for k in range(KH):
                        if m == 0:
                            pe.wait_ge(h1_split, KH * b + k + 1)
                        mm = split_products(ps_h[m % 2][:, :], wh2_hi[:, m, k * P:(k + 1) * P],
                                            wh2_lo[:, m, k * P:(k + 1) * P], h1_hi[par][:, k, :],
                                            h1_lo[par][:, k, :], k == 0, k == KH - 1)
                    mm.then_inc(h2_mm, 1)
                    if first and m == 1:
                        pe.wait_ge(w3_in, 16 * 2 * KH)
                    if m >= 1:
                        third(b, m - 1)
                    elif not first:
                        third(b - 1, KH - 1)
                    if m == 1 and not first:
                        to_rows(b - 1)

            over_blocks(pe, phase_c)
            third(NB - 1, KH - 1)
            to_rows(NB - 1)

        @block.scalar
        def _(act):
            def stage_v(b, par, t):
                act.wait_ge(qkv_done, NT * b + t + 1)
                wait_count(act, head_done, STEPS * (b - 1) - NT + t + 1)
                act.activation(v_s[par][:, t, :, 0:HD], ps_v[:, 0:D].rearrange("p (h d) -> p h d", d=HD),
                               ACT.Copy).then_inc(v_read, 1)

            def stack_out(b, par, g, in_turn=(ps_stack,)):
                t, part = STACK_ORDER[g]
                dst = (qT, kT)[part % 2][par]
                act.wait_ge(stackT_done, NST * NT * b + g + 1)
                if g == 0:
                    wait_count(act, score_done, 2 * STEPS * (b - 1))
                act.activation(dst[:, 4 * (part // 2):4 * (part // 2) + 4, t * P:(t + 1) * P],
                               in_turn[g % len(in_turn)][:, :].rearrange("p (j n) -> p j n", n=P), ACT.Copy).then_inc(stackT_read, 1)

            def copy_scores(b, s):
                for r in range(2):
                    act.wait_ge(score_done, 2 * (STEPS * b + s) + r + 1)
                    wait_count(act, exp_done, STEPS * b + s - 1)
                    act.activation(merged_s[s % 2][:, r::2, :],
                                   ps_score[r][:, :].rearrange("p (h n) -> p h n", h=2)[:, :, P:2 * P],
                                   ACT.Copy).then_inc(copied, 1)

            def exponentials(b, s):
                act.wait_ge(low_ready, STEPS * b + s + 1)
                wait_count(act, probT_done, STEPS * b + s - 1)
                for c in range(GH):
                    a = act.activation(prob[s % 2][:, c, :], merged_s[s % 2][:, c, :], ACT.Exp,
                                       bias=low[s % 2][:, c:c + 1], scale=-1.0)
                a.then_inc(exp_done, 1)

            def turned_out(b, s):
                act.wait_ge(probT_done, STEPS * b + s + 1)
                wait_count(act, lower_ready, STEPS * b + s - 1)
                wait_count(act, upper_ready, uppers(b, s - 2))
                act.activation(turned[s % 2][:].rearrange("p c n -> p (c n)"), ps_probT[:, :],
                               ACT.Copy).then_inc(turned_ready, 1)

            def head_out(b, s, first, flush):
                if s not in TO_TOKENS or not uses_shared(s, first, flush):
                    return
                back, hg = TO_TOKENS[s]
                act.wait_ge(head_done, STEPS * (b + back) + NT * hg + NT)
                if s == 0:
                    act.wait_ge(shared_done, shared_uses(b, 0, first, flush))
                elif uses_shared(s - NT, first, flush):
                    act.wait_ge(shared_done, shared_uses(b, s - NT, first, flush) + 1)
                act.activation(headT[:, :], ps_head[:, :], ACT.Copy).then_inc(head_read, 1)

            def shared(b, s, first, flush):
                if first or s not in (5, 6, 14, 15):
                    return
                act.wait_ge(shared_done, shared_uses(b, s, first, flush) + 1)
                if s in (5, 6):
                    act.activation(attT_hi[:, s - 5, :], ps_shared[:, :], ACT.Copy).then_inc(shared_hi, 1)
                else:
                    if s == 14:
                        act.wait_ge(x1T_out, 16 * b)
                    act.activation(x1T_s[:, s - 14, :], ps_shared[:, :], ACT.Copy).then_inc(shared_read, 1)

            def phase_a(b, par, first, last):
                for s in range(STEPS):
                    if s % NT:
                        copy_scores(b, s)
                    if s >= 1:
                        exponentials(b, s - 1)
                    elif not first:
                        exponentials(b - 1, s - 1 + STEPS)
                    head_out(b, s, first, False)
                    if s >= 2:
                        turned_out(b, s - 2)
                    elif not first:
                        turned_out(b - 1, s - 2 + STEPS)
                    if s in STACK_STEP and not last:
                        stack_out(b + 1, 1 - par, STACK_STEP[s])
                    if s in LATE_STACK:
                        stack_out(b, par, LATE_STACK[s])
                    if s in QKV_STEP and not last:
                        stage_v(b + 1, 1 - par, QKV_STEP[s])
                    shared(b, s, first, False)

            act.wait_ge(wattn_in[0], 16)
            act.activation(wq_hi[:, 0], wq_f[:, 0], ACT.Copy).then_inc(wattn_hi, 1)
            act.wait_ge(wattn_in[1], 16)
            act.activation(wq_hi[:, 1], wq_f[:, 1], ACT.Copy).then_inc(wattn_hi, 1)
            act.wait_ge(wattn_in[2], 16)
            act.activation(wo_hi[:], wo_f[:], ACT.Copy).then_inc(wattn_hi, 1)
            for t in range(NT):
                stage_v(0, 0, t)
                for g in range(max(NST * (t - 1), 0), min(NST * t, LATE_STACK[0])):
                    stack_out(0, 0, g, SETUP_BANKS)
            over_blocks(act, phase_a)
            for s in range(FLUSH_STEPS):
                if s == 0:
                    exponentials(NB - 1, STEPS - 1)
                if s < 2:
                    turned_out(NB - 1, s - 2 + STEPS)
                head_out(NB, s, False, True)
                shared(NB, s, False, True)

            def split_bx(b):
                act.wait_ge(bx_in, 16 * (b + 1))
                wait_count(act, up_done, KH * b)
                act.activation(bx_hi[:], bx_s[:], ACT.Copy).then_inc(bx_hi_ready, 1)

            def h0_high(b, m):
                act.wait_ge(h0_ready, KH * b + m + 1)
                wait_count(act, h1_mm, KH * b)
                act.activation(h0_hi[:, m, :], h0_s[m % 2][:], ACT.Copy).then_inc(h0_hi_ready, 1)

            def phase_b(b, last):
                for m in range(KH):
                    act.wait_ge(gate_done, KH * b + m + 1)
                    wait_count(act, h0_ready, KH * b + m - 1)
                    act.activation(silu_s[m % 2][:], ps_gate[m % 2][:, :], ACT.Silu,
                                   scale=s1_s[:, m:m + 1]).then_inc(silu_ready, 1)
                    if m:
                        h0_high(b, m - 1)
                h0_high(b, KH - 1)
                for m in range(KH):
                    act.wait_ge(h1_mm, KH * b + m + 1)
                    wait_count(act, h1_out[m % 2], 16 * (KH // 2 * b + m // 2))
                    act.activation(h1_s[m % 2][:], ps_h[m % 2][:, :], ACT.Gelu,
                                   scale=sh1_s[:, m:m + 1]).then_inc(h1_ready, 1)
                    if m == 1 and not last:
                        split_bx(b + 1)

            split_bx(0)
            phase_b(0, False)
            with act.Fori(1, NB - 1) as b:
                phase_b(b, False)
            phase_b(NB - 1, True)

            def split_h1(b, par, k):
                act.wait_ge(h1_in_s[k % 4], 16 * (KH // 4 * b + k // 4 + 1))
                wait_count(act, h2_mm, KH * (b - 1))
                act.activation(h1_hi[par][:, k, :], h1_in[k % 4][:], ACT.Copy).then_inc(h1_hi_ready, 1)

            def out_features(b):
                act.wait_ge(w3_done, KH * (b + 1))
                for kc in range(KD):
                    act.activation(oT_s[:, kc, :], ps_oT[kc][:, :], ACT.Copy,
                                   scale=s3_s[:, kc:kc + 1]).then_inc(oT_ready, 1)

            def phase_c(b, par, first, last):
                for m in range(KH):
                    act.wait_ge(h2_mm, KH * b + m + 1)
                    wait_count(act, h2_split, KH * b + m - 1)
                    act.activation(h2_s[m % 2][:], ps_h[m % 2][:, :], ACT.Gelu,
                                   scale=sh2_s[:, m:m + 1]).then_inc(h2_ready, 1)
                    act.wait_ge(h2_ready, KH * b + m + 1)
                    wait_count(act, w3_done, KH * b + m - 1)
                    act.activation(h2_hi[m % 2][:], h2_s[m % 2][:], ACT.Copy).then_inc(h2_hi_ready, 1)
                    if m == 0 and not first:
                        out_features(b - 1)
                    if not last:
                        split_h1(b + 1, 1 - par, m)

            for k in range(KH):
                split_h1(0, 0, k)
            over_blocks(act, phase_c)
            out_features(NB - 1)

        @block.vector
        def _(dve):
            dve.memset(neg_half[:], -0.5).then_inc(const_set, 1)
            for st in stack:
                dve.memset(st[:, :, 3, :].bitcast(F32), 0.0).then_inc(const_set, 1)
            for v in v_s:
                dve.memset(v[:, :, :, HD:2 * HD], 1.0).then_inc(const_set, 1)
            dve.wait_ge(const_in, 16 * N_CONST)
            dve.tensor_copy(ident_r[:], ident_s[:]).then_inc(const_set, 1)
            dve.tensor_scalar(take_s[:], bias_s[:], 1.0, None, ALU.is_gt).then_inc(const_set, 1)
            dve.wait_ge(const_set, 7)

            def split_x(b):
                dve.wait_ge(xT_in, 16 * (b + 1))
                wait_count(dve, qkv_done, NT * b)
                dve.tensor_copy(xT_hi[:], xT_s[:]).then_inc(xT_hi_ready, 1)

            def stage_hi(b, t):
                dve.wait_ge(rope_sum, NT * b + t + 1)
                wait_count(dve, stackT_done, STEPS * (b - (t < 2)) + STACKS_OF_TILE[t - 2])
                st = stack[t % 2]
                src = qk_s[t % 2][:].rearrange("p (h d) -> p h d", d=HD)
                dve.tensor_copy(st[:, :, 0, :], src).then_inc(stack_hi, 1)
                dve.tensor_copy(st[:, 0:H, 1, :], src[:, 0:H, :]).then_inc(stack_hi2, 1)
                dve.tensor_copy(st[:, H:2 * H, 2, :], src[:, H:2 * H, :]).then_inc(stack_hi2, 1)

            def rope(b, t):
                dve.wait_ge(qkv_done, NT * b + t + 1)
                wait_count(dve, rope_sum, NT * b + t)
                x4 = ps_qk[:, :].rearrange("p (q h d) -> p q h d", q=2, d=HD)
                b4 = rope_b[:].rearrange("p (q h d) -> p q h d", q=2, d=HD)
                a3 = rope_a[:].rearrange("p (q g e) -> p q g e", q=2, e=HALF)
                x3 = ps_qk[:, :].rearrange("p (q g e) -> p q g e", q=2, e=HALF)
                dve.tensor_tensor(a3, x3, cos_s[:, t].unsqueeze(2).broadcast_to([P, 2, 2 * H, HALF]),
                                  ALU.mult).then_inc(rope_terms, 1)
                dve.tensor_tensor(b4[:, :, :, 0:HALF], x4[:, :, :, HALF:HD],
                                  nsin_s[:, t].unsqueeze(2).broadcast_to([P, 2, H, HALF]),
                                  ALU.mult).then_inc(rope_terms, 1)
                dve.tensor_tensor(b4[:, :, :, HALF:HD], x4[:, :, :, 0:HALF],
                                  sin_s[:, t].unsqueeze(2).broadcast_to([P, 2, H, HALF]),
                                  ALU.mult).then_inc(qk_read, 1)

            def merge(b, s):
                for r in range(2):
                    dst = merged_s[s % 2][:, r::2, :]
                    src = ps_score[r][:, :].rearrange("p (h n) -> p h n", h=2)[:, :, 0:P]
                    if s % NT == 0:
                        dve.wait_ge(score_done, 2 * (STEPS * b + s) + r + 1)
                        wait_count(dve, exp_done, STEPS * b + s - 1)
                        dve.tensor_tensor(dst, src, bias_s[:].unsqueeze(1).broadcast_to([P, 2, P]),
                                          ALU.add).then_inc(merged, 1)
                    else:
                        dve.wait_ge(copied, 2 * (NT - 1) * (NG * b + s // NT) + 2 * (s % NT - 1) + r + 1)
                        dve.nop(nofuse=True)
                        dve.copy_predicated(dst, take_s[:].unsqueeze(1).broadcast_to([P, 2, P]),
                                            src).then_inc(merged, 1)
                dve.wait_ge(merged, 2 * (STEPS * b + s) + 2)
                wait_count(dve, exp_done, STEPS * b + s - 1)
                dve.tensor_reduce(low[s % 2][:], merged_s[s % 2][:], AX.X, ALU.min).then_inc(low_ready, 1)

            def lower_probs(b, s):
                dve.wait_ge(turned_ready, STEPS * b + s + 1)
                wait_count(dve, head_done, STEPS * b + s - NT + 1)
                dve.tensor_tensor(probT[s % NT][:, :, 0:P], turned[s % 2][:],
                                  lower_s[:].unsqueeze(1).broadcast_to([P, GH, P]), ALU.mult).then_inc(lower_ready, 1)

            def normalise(b, hg, no):
                dve.wait_ge(shared_done, no + 1)
                sums = ps_shared[:, :].rearrange("p (t c e) -> p t c e", c=GH, e=2 * HD)
                dve.reciprocal(denom[:], sums[:, :, :, HD]).then_inc(denom_ready, 1)
                dve.wait_ge(denom_ready, NG * b + hg + 1)
                dst = att[:].rearrange("p t (g c d) -> p t g c d", g=NG, d=HD)[:, :, hg]
                dve.tensor_tensor(dst, sums[:, :, :, 0:HD], denom[:].unsqueeze(3).broadcast_to([P, NT, GH, HD]),
                                  ALU.mult).then_inc(shared_read, 1)

            def residual(b, par, pair, no):
                dve.wait_ge(shared_done, no + 1)
                if pair == 0:
                    dve.wait_ge(x_in, 16 * (b + 1))
                    dve.wait_ge(x1_out, 16 * (b + 1))
                r = res[:, 2 * pair:2 * pair + 2, :]
                dve.tensor_tensor(r, ps_shared[:, :].rearrange("p (t d) -> p t d", t=2),
                                  x_s[par][:, 2 * pair:2 * pair + 2, :], ALU.add).then_inc(shared_read, 1)
                dve.wait_ge(shared_read, no + 1)
                statistics(res, pair, b, stats_ready, mean_ready)

            def statistics(src, pair, b, stats_sem, mean_sem):
                for u in range(2):
                    dve.bn_stats(stats[:, 2 * pair + u, :], src[:, 2 * pair + u, :]).then_inc(stats_sem, 1)
                dve.wait_ge(stats_sem, 2 * (2 * b + pair) + 2)
                dve.nop(nofuse=True)
                for u in range(2):
                    dve.bn_aggr(meanvar[:, 2 * pair + u, :], stats[:, 2 * pair + u, :]).then_inc(mean_sem, 1)

            def normed(src, dst, pair, b, rstd_sem, ready):
                dve.wait_ge(rstd_sem, 2 * b + pair + 1)
                for u in range(2):
                    t = 2 * pair + u
                    op = dve.tensor_scalar(dst[:, t, :], src[:, t, :], meanvar[:, t, 0:1], rstd[:, t:t + 1],
                                           ALU.subtract, ALU.mult)
                op.then_inc(ready, 1)

            def shared(b, par, s, first, flush):
                if not uses_shared(s, first, flush):
                    return
                no = shared_uses(b, s, first, flush)
                if s in TO_TOKENS:
                    back, hg = TO_TOKENS[s]
                    normalise(b + back, hg, no)
                elif s in (5, 6):
                    dve.wait_ge(shared_hi, KD * (b - 1) + s - 4)
                    dve.tensor_tensor(attT_lo[:, s - 5, :], ps_shared[:, :], attT_hi[:, s - 5, :].bitcast(F32),
                                      ALU.subtract).then_inc(shared_read, 1)
                elif s in (9, 10):
                    residual(b - 1, 1 - par, s - 9, no)

            def phase_a(b, par, first, last):
                for s in range(STEPS):
                    if s == 0 and not last:
                        split_x(b + 1)
                    merge(b, s)
                    if s >= 3:
                        lower_probs(b, s - 3)
                    elif not first:
                        lower_probs(b - 1, s - 3 + STEPS)
                    if s in (12, 13) and not first:
                        normed(res, res, s - 12, b - 1, rstd_ready, x1_ready)
                    if s - 1 in QKV_STEP and not last:
                        rope(b + 1, QKV_STEP[s - 1])
                    if s - 2 in QKV_STEP and not last:
                        stage_hi(b + 1, QKV_STEP[s - 2])
                    shared(b, par, s, first, False)

            split_x(0)
            for kc in range(KD):
                dve.wait_ge(wattn_hi, kc + 1)
                dve.tensor_tensor(wq_lo[:, kc], wq_f[:, kc], wq_hi[:, kc].bitcast(F32),
                                  ALU.subtract).then_inc(wattn_split, 1)
            dve.wait_ge(wattn_hi, 3)
            dve.tensor_tensor(wo_lo[:], wo_f[:], wo_hi[:].bitcast(F32), ALU.subtract).then_inc(wattn_split, 1)
            for t in range(NT):
                rope(0, t)
                stage_hi(0, t)
            over_blocks(dve, phase_a)
            for s in range(FLUSH_STEPS):
                if s < 3:
                    lower_probs(NB - 1, s - 3 + STEPS)
                if s in (12, 13):
                    normed(res, res, s - 12, NB - 1, rstd_ready, x1_ready)
                shared(NB, 0, s, False, True)

            def split_bx(b):
                dve.wait_ge(bx_hi_ready, b + 1)
                dve.tensor_tensor(bx_lo[:], bx_s[:], bx_hi[:].bitcast(F32), ALU.subtract).then_inc(bx_ready, 1)

            def h0_low(b, m):
                dve.wait_ge(h0_hi_ready, KH * b + m + 1)
                dve.tensor_tensor(h0_lo[:, m, :], h0_s[m % 2][:], h0_hi[:, m, :].bitcast(F32),
                                  ALU.subtract).then_inc(h0_split, 1)

            def phase_b(b, last):
                for m in range(KH):
                    dve.wait_ge(up_done, KH * b + m + 1)
                    dve.wait_ge(silu_ready, KH * b + m + 1)
                    wait_count(dve, h0_split, KH * b + m - 1)
                    dve.scalar_tensor_tensor(h0_s[m % 2][:], ps_up[m % 2][:, :], s2_s[:, m:m + 1],
                                             silu_s[m % 2][:], ALU.mult, ALU.mult).then_inc(h0_ready, 1)
                    if m:
                        h0_low(b, m - 1)
                h0_low(b, KH - 1)
                if not last:
                    split_bx(b + 1)

            split_bx(0)
            phase_b(0, False)
            with dve.Fori(1, NB - 1) as b:
                phase_b(b, False)
            phase_b(NB - 1, True)

            def split_h1(b, par, k):
                dve.wait_ge(h1_hi_ready, KH * b + k + 1)
                dve.tensor_tensor(h1_lo[par][:, k, :], h1_in[k % 4][:], h1_hi[par][:, k, :].bitcast(F32),
                                  ALU.subtract).then_inc(h1_split, 1)

            def out_rows(b, pair):
                dve.wait_ge(yT_done, 2 * b + pair + 1)
                if pair == 0:
                    dve.wait_ge(x1_in, 16 * (b + 1))
                    dve.wait_ge(y_out, 16 * (b + 1))
                dve.tensor_tensor(y_s[:, 2 * pair:2 * pair + 2, :], ps_y[pair][:, :].rearrange("p (t d) -> p t d", t=2),
                                  x1_s[:, 2 * pair:2 * pair + 2, :], ALU.add).then_inc(y_sum, 1)
                dve.wait_ge(y_sum, 2 * b + pair + 1)
                statistics(y_s, pair, b, cstats_ready, cmean_ready)

            def phase_c(b, par, first, last):
                for m in range(KH):
                    dve.wait_ge(h2_hi_ready, KH * b + m + 1)
                    dve.tensor_tensor(h2_lo[m % 2][:], h2_s[m % 2][:], h2_hi[m % 2][:].bitcast(F32),
                                      ALU.subtract).then_inc(h2_split, 1)
                    if not last:
                        split_h1(b + 1, 1 - par, m)
                    if not first and m in (1, 2):
                        out_rows(b - 1, m - 1)
                    if not first and m in (3, 4):
                        normed(y_s, y_s, m - 3, b - 1, crstd_ready, y_ready)

            for k in range(KH):
                split_h1(0, 0, k)
            over_blocks(dve, phase_c)
            for pair in range(2):
                out_rows(NB - 1, pair)
            for pair in range(2):
                normed(y_s, y_s, pair, NB - 1, crstd_ready, y_ready)

        @block.gpsimd
        def _(pool):
            def split_x(b):
                pool.wait_ge(xT_hi_ready, b + 1)
                pool.tensor_tensor(xT_lo[:], xT_s[:], xT_hi[:].bitcast(F32), ALU.subtract).then_inc(xT_ready, 1)

            def rotate(b, t):
                pool.wait_ge(rope_terms, 2 * (NT * b + t + 1))
                pool.wait_ge(qk_read, NT * b + t + 1)
                wait_count(pool, stack_hi2, 2 * (NT * b + t - 1))
                wait_count(pool, stack_lo, 2 * (NT * b + t - 1))
                pool.tensor_tensor(qk_s[t % 2][:], rope_a[:], rope_b[:], ALU.add).then_inc(rope_sum, 1)

            def upper_probs(b, s):
                if s % NT == 0:
                    return
                pool.wait_ge(turned_ready, STEPS * b + s + 1)
                wait_count(pool, head_done, STEPS * b + s - NT)
                pool.tensor_tensor(probT[s % NT - 1][:, :, P:2 * P], turned[s % 2][:],
                                   upper_s[:].unsqueeze(1).broadcast_to([P, GH, P]), ALU.mult).then_inc(upper_ready, 1)

            def stack_low(b, t):
                st = stack[t % 2]
                src = qk_s[t % 2][:].rearrange("p (h d) -> p h d", d=HD)
                pool.wait_ge(stack_hi, NT * b + t + 1)
                pool.tensor_tensor(st[:, 0:H, 2, :], src[:, 0:H, :], st[:, 0:H, 0, :].bitcast(F32),
                                   ALU.subtract).then_inc(stack_lo, 1)
                pool.tensor_tensor(st[:, H:2 * H, 1, :], src[:, H:2 * H, :], st[:, H:2 * H, 0, :].bitcast(F32),
                                   ALU.subtract).then_inc(stack_lo, 1)

            def split_piece(b, q):
                pool.wait_ge(piece_in[q % 2], 16 * (NPIECE // 2 * b + q // 2 + 1))
                wait_count(pool, piece_out, 32 * (NPIECE * b + q))
                pool.nop(nofuse=True)
                pool.tensor_scalar(piece_hi[:], piece[q % 2][:], 1.0, 1.0, ALU.mult, ALU.mult).then_inc(piece_hi_ready, 1)
                pool.wait_ge(piece_hi_ready, NPIECE * b + q + 1)
                pool.tensor_tensor(piece_lo[:], piece[q % 2][:], piece_hi[:].bitcast(F32),
                                   ALU.subtract).then_inc(piece_lo_ready, 1)

            def inverse_deviation(b, pair, mean_sem, step, ready):
                n = 5 * (2 * b + pair)
                ab = slice(2 * pair, 2 * pair + 2)
                v, y, t, r = vareps[:, ab], rstd0[:, ab], rsq[:, ab], rstd[:, ab]
                pool.wait_ge(mean_sem, 2 * (2 * b + pair) + 2)
                pool.nop(nofuse=True)
                pool.tensor_scalar(v, meanvar[:, ab, 1], EPS, None, ALU.add).then_inc(step, 1)
                pool.wait_ge(step, n + 1)
                pool.tensor_tensor(y, v, neg_half[:, ab], ALU.pow).then_inc(step, 1)
                pool.wait_ge(step, n + 2)
                pool.tensor_tensor(t, y, y, ALU.mult).then_inc(step, 1)
                pool.wait_ge(step, n + 3)
                pool.tensor_tensor(t, t, v, ALU.mult).then_inc(step, 1)
                pool.wait_ge(step, n + 4)
                pool.nop(nofuse=True)
                pool.tensor_scalar(t, t, -0.5, 1.5, ALU.mult, ALU.add).then_inc(step, 1)
                pool.wait_ge(step, n + 5)
                pool.tensor_tensor(r, y, t, ALU.mult).then_inc(ready, 1)

            def phase_a(b, par, first, last):
                for s in range(STEPS):
                    if s == 0 and not last:
                        split_x(b + 1)
                    if s >= 3:
                        upper_probs(b, s - 3)
                    elif not first:
                        upper_probs(b - 1, s - 3 + STEPS)
                    if s in (10, 11) and not first:
                        inverse_deviation(b - 1, s - 10, mean_ready, rstd_step, rstd_ready)
                    if s - 1 in QKV_STEP and not last:
                        rotate(b + 1, QKV_STEP[s - 1])
                    if s - 2 in QKV_STEP and not last:
                        stack_low(b + 1, QKV_STEP[s - 2])
                    if s in PIECE_STEP:
                        split_piece(b, PIECE_STEP[s])

            split_x(0)
            for t in range(NT):
                rotate(0, t)
                stack_low(0, t)
            pool.wait_ge(const_in, 16 * N_CONST)
            over_blocks(pool, phase_a)
            for s in range(3):
                upper_probs(NB - 1, s - 3 + STEPS)
            for pair in range(2):
                inverse_deviation(NB - 1, pair, mean_ready, rstd_step, rstd_ready)
            with pool.Fori(0, NB) as b:
                for pair in range(2):
                    inverse_deviation(b, pair, cmean_ready, crstd_step, crstd_ready)


def constants():
    theta = (1.0 / 10000.0 ** (np.arange(HALF, dtype=np.float32) / HALF)).astype(np.float32)
    freqs = np.arange(TB, dtype=np.float32)[:, None] * theta[None, :]
    by_tile = lambda a: np.ascontiguousarray(a.reshape(NT, P, HALF).transpose(1, 0, 2))
    scale = np.array([-1.0 / np.sqrt(HD), 1.0], np.float32)[None, None, :, None]
    cos = by_tile(np.cos(freqs).astype(np.float32))[:, :, None, :] * scale
    sin = by_tile(np.sin(freqs).astype(np.float32))[:, :, None, :] * scale
    row, col = np.arange(P)[:, None], np.arange(P)[None, :]
    return {
        "cos": cos,
        "sin": np.stack([sin, -sin]),
        "lower": (row <= col).astype(np.float32),
        "upper": (row > col).astype(np.float32),
        "bias": np.where(col > row, np.float32(MASKED), np.float32(0)),
        "ident": np.eye(P, dtype=np.float32),
    }


def kernel(**inputs):
    import concourse.bacc as bacc
    from concourse.bass_utils import run_bass_kernel_spmd

    a = {k.removeprefix("L0_"): np.asarray(v) for k, v in inputs.items()}
    flat = a["attn_x"].reshape(NB * TB, D)

    def chunks(w, k):
        return w.reshape(-1, P, k, P).transpose(0, 3, 2, 1)

    packed = np.concatenate(
        [chunks(a["ffn_w1_w"], KD).reshape(KH, P, -1), chunks(a["ffn_w2_w"], KD).reshape(KH, P, -1),
         chunks(a["ffn_h1_w"], KH).reshape(KH, P, -1), chunks(a["ffn_h2_w"], KH).reshape(KH, P, -1),
         a["ffn_w3_w"].T.reshape(KH, P, D)], axis=2)
    by_chunk = lambda s: s.reshape(-1, P).T
    arrays = {
        "x": flat,
        "xT": flat.reshape(NB, TB, KD, P).transpose(0, 3, 2, 1),
        "wqkv": a["attn_Wqkv"].reshape(KD, P, 3 * D).transpose(1, 0, 2),
        "wout": a["attn_Wout"].reshape(KD, P, D).transpose(1, 0, 2),
        "wffn": packed,
        "s1": by_chunk(a["ffn_w1_s"]), "s2": by_chunk(a["ffn_w2_s"]),
        "sh1": by_chunk(a["ffn_h1_s"]), "sh2": by_chunk(a["ffn_h2_s"]), "s3": by_chunk(a["ffn_w3_s"]),
    } | constants()
    nc = bacc.Bacc("TRN2", target_bir_lowering=False, num_devices=1)
    feed, args = {}, {}
    for name, array in arrays.items():
        array = np.ascontiguousarray(array)
        feed[f"in_{name}"] = array
        args[name] = nc.dram_tensor(f"in_{name}", array.shape, mybir.dt.from_np(array.dtype), kind="ExternalInput").ap()
    out = nc.dram_tensor("out_0", (NB * TB, D), F32, kind="ExternalOutput").ap()
    build(nc, out=out, **args)
    r = run_bass_kernel_spmd(nc, [feed], core_ids=[0])
    return r.results[0]["out_0"].reshape(NB, TB, D)
```

```python
from contextlib import ExitStack

import numpy as np

import concourse.bass as bass
from concourse import mybir

ALU = mybir.AluOpType
ACT = mybir.ActivationFunctionType
AX = mybir.AxisListType
F32 = mybir.dt.float32
F32R = mybir.dt.float32r
U8 = mybir.dt.uint8

P = 128
NB = 8
TB = 512
NT = TB // P
D = 256
KD = D // P
H = 16
HD = D // H
HALF = HD // 2
HID = 1024
KH = HID // P
WINDOW = 128
EPS = 1e-5

assert WINDOW == P

GH = 4
NG = H // GH
STEPS = NG * NT
SLOT = 64
PARTS = 3 * HD
NST = 4
MASKED = 3e38
GLU_COLS = 2 * KD * P
HID_COLS = KH * P
W3_COLS = D
H1_AT = GLU_COLS
H2_AT = H1_AT + HID_COLS
W3_AT = H2_AT + HID_COLS
PACK = W3_AT + W3_COLS
PIECE_B = H2_AT // 2
PIECE_C = (PACK - H2_AT) // 2

QKV_STEP = {2: 0, 5: 1, 8: 2, 12: 3}
STACK_ORDER = [(0, 0), (0, 1), (0, 2), (0, 3), (1, 0), (1, 1), (1, 2), (1, 3),
               (2, 0), (2, 1), (3, 0), (3, 1), (2, 2), (2, 3), (3, 2), (3, 3)]
STACKS_BEFORE_SCORES = (2, 6, 10, 12)
STACKS_OF_TILE = (4, 8, 14, 16)
STACK_LAG = 6
STACK_STEP = {s: s - STACK_LAG for s in range(STACK_LAG, STEPS)}
LATE_STACK = {s: STEPS - STACK_LAG + s for s in range(STACK_LAG)}
SHARED_STEPS = (0, 4, 5, 6, 8, 9, 10, 12, 14, 15)
FIRST_SHARED_STEPS = (8, 12)
FLUSH_SHARED_STEPS = (0, 4, 5, 6, 9, 10, 14, 15)
FLUSH_STEPS = 16
TO_TOKENS = {0: (-1, 2), 4: (-1, 3), 8: (0, 0), 12: (0, 1)}
PIECE_STEP = {1: (0, 0), 5: (0, 1), 8: (1, 0), 12: (1, 1)}


def shared_uses(b, s, first, flush):
    if first:
        return FIRST_SHARED_STEPS.index(s)
    before_block = len(SHARED_STEPS) * (b - 1) + len(FIRST_SHARED_STEPS)
    return before_block + (FLUSH_SHARED_STEPS if flush else SHARED_STEPS).index(s)


def uses_shared(s, first, flush):
    return s in (FIRST_SHARED_STEPS if first else FLUSH_SHARED_STEPS if flush else SHARED_STEPS)


def later_tiles(b, s):
    return (NT - 1) * (NG * b + s // NT) + s % NT


def wait_count(eng, sem, count):
    if not isinstance(count, int) or count > 0:
        eng.wait_ge(sem, count)


def over_blocks(eng, block, peeled=1):
    block(0, 0, True, False)
    with eng.Fori(0, (NB - 1 - peeled) // 2) as pair:
        for j in (1, 2):
            block(pair * 2 + j, j % 2, False, False)
    for b in range(NB - peeled, NB):
        block(b, b % 2, False, b == NB - 1)


def build(nc, x, xT, wqkv, wout, wffn, s1, s2, sh1, sh2, s3, cos, sin, lower, upper, bias, ident, out):
    x_v = x.rearrange("(b t p) d -> b p t d", b=NB, t=NT)
    out_v = out.rearrange("(b t p) d -> b p t d", b=NB, t=NT)
    with ExitStack() as ctx:
        def scratch(name, shape, dt=F32):
            return nc.dram_tensor(name, shape, dt, kind="Internal").ap()

        w_hi_d = scratch("w_hi_d", (NB, P, PACK))
        w_lo_d = scratch("w_lo_d", (NB, P, PACK))
        x1_d = scratch("x1_d", (NB, P, NT, D))
        x1T_d = scratch("x1T_d", (NB, P, KD, TB))
        h1_d = scratch("h1_d", (NB, P, KH, TB))

        cursor = [(nc.sbuf_base + 63) // 64 * 64]

        def sb(name, shape, dt=F32):
            size = int(np.prod(shape[1:])) * (1 if dt == U8 else 4)
            at = cursor[0]
            cursor[0] += (size + 31) // 32 * 32
            return nc.alloc_sbuf_tensor_at(name, shape, dt, offset=at)

        def bank(name):
            return ctx.enter_context(nc.psum_tensor(name, [P, 512], F32))

        def sem(name):
            return ctx.enter_context(nc.semaphore(name))

        s1_s, s2_s, sh1_s, sh2_s = (sb(n, [P, KH]) for n in ("s1_s", "s2_s", "sh1_s", "sh2_s"))
        s3_s = sb("s3_s", [P, KD])
        ident_s = sb("ident_s", [P, P])
        neg_half = sb("neg_half", [P, 4])
        stats = sb("stats", [P, 4, 6])
        meanvar = sb("meanvar", [P, 4, 2])
        vareps, rstd0, rsq, rstd = (sb(n, [P, 4]) for n in ("vareps", "rstd0", "rsq", "rstd"))
        phase_base = cursor[0]

        x_s = [sb(f"x_s{i}", [P, NT, D]) for i in range(2)]
        wo_hi, wo_lo = sb("wo_hi", [P, KD, D], F32R), sb("wo_lo", [P, KD, D], F32R)
        att, res = sb("att", [P, NT, D]), sb("res", [P, NT, D])
        attT_hi, attT_lo = sb("attT_hi", [P, KD, TB], F32R), sb("attT_lo", [P, KD, TB], F32R)
        x1T_s = sb("x1T_s", [P, KD, TB])
        zone_glu = cursor[0]
        qT, kT = [None, None], [None, None]
        qT[0], kT[0] = sb("qT0", [P, H // 2, TB], F32R), sb("kT0", [P, H // 2, TB], F32R)
        zone_h1_hi = cursor[0]
        qT[1], kT[1] = sb("qT1", [P, H // 2, TB], F32R), sb("kT1", [P, H // 2, TB], F32R)
        zone_h1_lo = cursor[0]
        v_s = [None, sb("v1", [P, NT, H, 2 * HD])]
        merged_s = [sb(f"merged_s{i}", [P, GH, P]) for i in range(2)]
        prob = [sb(f"prob{i}", [P, GH, P]) for i in range(2)]
        wq_f = nc.alloc_sbuf_tensor_at("wq_f", [P, KD, 3 * D], F32, offset=cursor[0])
        wo_f = nc.alloc_sbuf_tensor_at("wo_f", [P, KD, D], F32, offset=cursor[0] + 4 * KD * 3 * D)
        probT = [sb(f"probT{j}", [P, GH, 2 * P]) for j in range(NT)]
        zone_tokens = cursor[0]
        xT_s = sb("xT_s", [P, KD, TB])
        xT_hi, xT_lo = sb("xT_hi", [P, KD, TB], F32R), sb("xT_lo", [P, KD, TB], F32R)
        wq_hi, wq_lo = sb("wq_hi", [P, KD, 3 * D], F32R), sb("wq_lo", [P, KD, 3 * D], F32R)
        rope_a, rope_b = sb("rope_a", [P, 2 * D]), sb("rope_b", [P, 2 * D])
        qk_s = [sb(f"qk_s{i}", [P, 2 * D]) for i in range(2)]
        stack = [sb(f"stack{i}", [P, 2 * H, 4, HD], F32R) for i in range(2)]
        v_s[0] = sb("v0", [P, NT, H, 2 * HD])
        turned = [sb(f"turned{i}", [P, GH, P]) for i in range(2)]
        zone_a = cursor[0]
        ident_r = sb("ident_r", [P, P], F32R)
        low = [sb(f"low{i}", [P, GH]) for i in range(2)]
        headT = sb("headT", [P, TB])
        denom = sb("denom", [P, NT, GH])
        cos_s, sin_s, nsin_s = (sb(n, [P, NT, 2, HALF]) for n in ("cos_s", "sin_s", "nsin_s"))
        lower_s, upper_s, bias_s = (sb(n, [P, P]) for n in ("lower_s", "upper_s", "bias_s"))
        take_s = sb("take_s", [P, P], U8)
        piece = [sb(f"piece{i}", [P, PIECE_B]) for i in range(2)]
        piece_hi, piece_lo = sb("piece_hi", [P, PIECE_B], F32R), sb("piece_lo", [P, PIECE_B], F32R)
        a_end = cursor[0]

        cursor[0] = phase_base
        wh2_hi = sb("wh2_hi", [P, KH, HID_COLS], F32R)
        assert cursor[0] <= zone_glu
        cursor[0] = zone_glu
        wglu_hi, wglu_lo = sb("wglu_hi", [P, KH, GLU_COLS], F32R), sb("wglu_lo", [P, KH, GLU_COLS], F32R)
        assert cursor[0] <= zone_h1_hi
        cursor[0] = zone_h1_hi
        wh1_hi = sb("wh1_hi", [P, KH, HID_COLS], F32R)
        assert cursor[0] <= zone_h1_lo
        cursor[0] = zone_h1_lo
        wh1_lo = sb("wh1_lo", [P, KH, HID_COLS], F32R)
        assert cursor[0] <= zone_tokens
        cursor[0] = zone_tokens
        bx_s = sb("bx_s", [P, KD, TB])
        bx_hi, bx_lo = sb("bx_hi", [P, KD, TB], F32R), sb("bx_lo", [P, KD, TB], F32R)
        after_bx = cursor[0] = max(cursor[0], zone_tokens + 4 * KH // 2 * HID_COLS)
        h0_hi, h0_lo = sb("h0_hi", [P, KH, TB], F32R), sb("h0_lo", [P, KH, TB], F32R)
        after_h0 = cursor[0]
        silu_s = [sb(f"silu_s{i}", [P, TB]) for i in range(2)]
        h0_s = [sb(f"h0_s{i}", [P, TB]) for i in range(2)]
        before_h1 = cursor[0]
        h1_s = [sb(f"h1_s{i}", [P, TB]) for i in range(2)]
        assert cursor[0] <= zone_a

        cursor[0] = zone_glu
        h1_hi, h1_lo = [None, None], [None, None]
        h1_hi[0], h1_lo[0] = sb("h1_hi0", [P, KH, TB], F32R), sb("h1_lo0", [P, KH, TB], F32R)
        assert cursor[0] <= zone_h1_hi
        cursor[0] = zone_tokens
        wh2_lo = [sb(f"wh2_lo{m}", [P, HID_COLS], F32R) for m in range(KH // 2)]
        assert cursor[0] <= after_bx
        cursor[0] = after_h0
        h1_in = [sb(f"h1_in{i}", [P, TB]) for i in range(4)]
        assert cursor[0] <= before_h1
        cursor[0] = zone_h1_hi
        h1_hi[1], h1_lo[1] = sb("h1_hi1", [P, KH, TB], F32R), sb("h1_lo1", [P, KH, TB], F32R)
        wh2_lo += [sb(f"wh2_lo{m}", [P, HID_COLS], F32R) for m in range(KH // 2, KH)]
        w3_hi, w3_lo = sb("w3_hi", [P, KH, D], F32R), sb("w3_lo", [P, KH, D], F32R)
        assert cursor[0] <= zone_tokens
        cursor[0] = after_bx
        h2_s = [sb(f"h2_s{i}", [P, TB]) for i in range(2)]
        h2_hi = [sb(f"h2_hi{i}", [P, TB], F32R) for i in range(2)]
        h2_lo = [sb(f"h2_lo{i}", [P, TB], F32R) for i in range(2)]
        oT_s = sb("oT_s", [P, KD, TB])
        x1_s = sb("x1_s", [P, NT, D])
        y_s = sb("y_s", [P, NT, D])
        assert cursor[0] <= after_h0
        assert a_end <= nc.sbuf_usable_end

        banks = [bank(f"bank{i}") for i in range(8)]
        ps_qk, ps_v, ps_stack = banks[0], banks[1], banks[2]
        ps_score = [banks[3], banks[4]]
        ps_probT, ps_head, ps_shared = banks[5], banks[6], banks[7]
        SETUP_BANKS = (ps_stack, ps_head)
        ps_gate, ps_up, ps_h = [banks[0], banks[1]], [banks[2], banks[3]], [banks[4], banks[5]]
        ps_oT = [banks[2], banks[3]]
        ps_y = [banks[6], banks[7]]

        N_CONST = 12
        const_in = sem("const_in")
        wattn_in = [sem("wq0_in"), sem("wq1_in"), sem("wo_in")]
        const_set = sem("const_set")
        wattn_hi = sem("wattn_hi")
        wattn_split = sem("wattn_split")
        xT_in, xT_hi_ready, xT_ready = sem("xT_in"), sem("xT_hi_ready"), sem("xT_ready")
        x_in = sem("x_in")
        qkv_done, qk_read, v_read = sem("qkv_done"), sem("qk_read"), sem("v_read")
        rope_terms, rope_sum = sem("rope_terms"), sem("rope_sum")
        stack_hi, stack_hi2, stack_lo = sem("stack_hi"), sem("stack_hi2"), sem("stack_lo")
        stackT_done, stackT_read = sem("stackT_done"), sem("stackT_read")
        score_done, copied, merged, low_ready = sem("score_done"), sem("copied"), sem("merged"), sem("low_ready")
        exp_done, probT_done, turned_ready = sem("exp_done"), sem("probT_done"), sem("turned_ready")
        lower_ready, upper_ready, first_ready = sem("lower_ready"), sem("upper_ready"), sem("first_ready")
        head_done, head_read = sem("head_done"), sem("head_read")
        shared_done, shared_read, shared_hi = sem("shared_done"), sem("shared_read"), sem("shared_hi")
        denom_ready = sem("denom_ready")
        stats_ready, mean_ready, rstd_step, rstd_ready = (
            sem("stats_ready"), sem("mean_ready"), sem("rstd_step"), sem("rstd_ready"))
        x1_ready, x1_out, x1T_out = sem("x1_ready"), sem("x1_out"), sem("x1T_out")
        piece_in = [sem("piece_in0"), sem("piece_in1")]
        piece_hi_ready, piece_lo_ready = sem("piece_hi_ready"), sem("piece_lo_ready")
        piece_out = sem("piece_out")
        wglu_in = [sem(f"wglu_in{m}") for m in range(KH)]
        wh1_in = [sem(f"wh1_in{m}") for m in range(KH)]
        bx_in, bx_hi_ready, bx_ready = sem("bx_in"), sem("bx_hi_ready"), sem("bx_ready")
        gate_done, up_done, silu_ready, h0_ready = (
            sem("gate_done"), sem("up_done"), sem("silu_ready"), sem("h0_ready"))
        h0_hi_ready, h0_split, h1_mm, h1_ready = sem("h0_hi_ready"), sem("h0_split"), sem("h1_mm"), sem("h1_ready")
        h1_out = [sem("h1_out0"), sem("h1_out1")]
        wh2_in = [sem(f"wh2_in{m}") for m in range(KH)]
        w3_in = sem("w3_in")
        h1_in_s = [sem(f"h1_in_s{i}") for i in range(4)]
        h1_hi_ready, h1_split = sem("h1_hi_ready"), sem("h1_split")
        h2_mm, h2_ready, h2_hi_ready, h2_split = sem("h2_mm"), sem("h2_ready"), sem("h2_hi_ready"), sem("h2_split")
        w3_done, oT_ready, yT_done, y_sum = sem("w3_done"), sem("oT_ready"), sem("yT_done"), sem("y_sum")
        cstats_ready, cmean_ready, crstd_step, crstd_ready = (
            sem("cstats_ready"), sem("cmean_ready"), sem("crstd_step"), sem("crstd_ready"))
        x1_in, y_ready, y_out = sem("x1_in"), sem("y_ready"), sem("y_out")

        block = ctx.enter_context(nc.Block())

        @block.sync
        def _(sp):
            sp.dma_start(wq_f[:, 0], wqkv[:, 0]).then_inc(wattn_in[0], 16)
            sp.dma_start(xT_s[:], xT[0]).then_inc(xT_in, 16)
            sp.dma_start(wq_f[:, 1], wqkv[:, 1]).then_inc(wattn_in[1], 16)
            sp.dma_start(wo_f[:], wout).then_inc(wattn_in[2], 16)
            for dst, src in ((ident_s, ident), (cos_s, cos), (sin_s, sin[0]), (nsin_s, sin[1]), (lower_s, lower),
                             (upper_s, upper), (bias_s, bias), (s1_s, s1), (s2_s, s2),
                             (sh1_s, sh1), (sh2_s, sh2), (s3_s, s3)):
                sp.dma_start(dst[:], src).then_inc(const_in, 16)

            def results(b, flush):
                sp.wait_ge(x1_ready, 2 * b + 2)
                sp.dma_start(x1_d[b], res[:]).then_inc(x1_out, 16)
                sp.wait_ge(shared_read, shared_uses(b + 1, 15, False, flush) + 1)
                sp.dma_start(x1T_d[b], x1T_s[:]).then_inc(x1T_out, 16)

            def load_bx(b):
                sp.wait_ge(bx_ready, b)
                sp.dma_start(bx_s[:], x1T_d[b]).then_inc(bx_in, 16)

            def load_xT(b):
                sp.wait_ge(xT_ready, b)
                sp.dma_start(xT_s[:], xT[b]).then_inc(xT_in, 16)

            def store_piece(chunk, q, for_c=False):
                done = chunk + NB if for_c else chunk
                at, n = (H2_AT + q * PIECE_C, PIECE_C) if for_c else (q * PIECE_B, PIECE_B)
                sp.wait_ge(piece_lo_ready, 4 * done + 2 * q + 2)
                sp.dma_start(w_hi_d[chunk, :, at:at + n], piece_hi[:, 0:n].bitcast(F32)).then_inc(piece_out, 16)
                sp.dma_start(w_lo_d[chunk, :, at:at + n], piece_lo[:, 0:n].bitcast(F32)).then_inc(piece_out, 16)

            def load_glu(m):
                sp.dma_start(wglu_hi[:, m, :].bitcast(F32), w_hi_d[m, :, 0:GLU_COLS]).then_inc(wglu_in[m], 16)
                sp.dma_start(wglu_lo[:, m, :].bitcast(F32), w_lo_d[m, :, 0:GLU_COLS]).then_inc(wglu_in[m], 16)

            def load_piece(chunk, q, for_c=False):
                done = chunk + NB if for_c else chunk
                at, n = (H2_AT + q * PIECE_C, PIECE_C) if for_c else (q * PIECE_B, PIECE_B)
                wait_count(sp, piece_lo_ready, 4 * done + 2 * q - 2)
                sp.dma_start(piece[q][:, 0:n], wffn[chunk, :, at:at + n]).then_inc(piece_in[q], 16)

            def phase_a(b, par, first, last):
                load_piece(b, 0)
                load_piece(b, 1)
                if not isinstance(b, int) or b < NB - 2:
                    load_xT(b + 2)
                wait_count(sp, x_in, 16 * b)
                sp.dma_start(x_s[par][:], x_v[b]).then_inc(x_in, 16)
                if last:
                    sp.wait_ge(xT_ready, NB)
                    sp.wait_ge(qkv_done, NT * NB)
                    sp.wait_ge(x1T_out, 16 * 2)
                    sp.dma_start(bx_s[:], x1T_d[0]).then_inc(bx_in, 16)
                    sp.wait_ge(score_done, 2 * STEPS * (NB - 1))
                    sp.wait_ge(piece_out, 16 * 4 * (NB - 1))
                store_piece(b, 0)
                if last:
                    for m in range(KH - 1):
                        load_glu(m)
                if not first:
                    results(b - 1, False)
                store_piece(b, 1)

            sp.sem_inc(x1_out, 16)
            sp.sem_inc(x1T_out, 16)
            sp.sem_inc(y_out, 16)
            load_xT(1)
            over_blocks(sp, phase_a, peeled=3)
            sp.wait_ge(piece_out, 16 * 4 * NB)
            load_glu(KH - 1)
            load_bx(1)
            sp.wait_ge(head_done, STEPS * NB)
            for m in range(KH):
                sp.dma_start(wh1_hi[:, m, :].bitcast(F32), w_hi_d[m, :, H1_AT:H2_AT]).then_inc(wh1_in[m], 16)
                sp.dma_start(wh1_lo[:, m, :].bitcast(F32), w_lo_d[m, :, H1_AT:H2_AT]).then_inc(wh1_in[m], 16)
            results(NB - 1, True)
            sp.wait_ge(x1T_out, 16 * (NB + 1))
            sp.wait_ge(x1_out, 16 * (NB + 1))

            def store_h1(b, m):
                sp.wait_ge(h1_ready, KH * b + m + 1)
                sp.dma_start(h1_d[b, :, m, :], h1_s[m % 2][:]).then_inc(h1_out[m % 2], 16)

            for m in range(KH):
                store_h1(0, m)
            load_bx(2)
            with sp.Fori(0, 2) as pair:
                for m in range(KH):
                    load_piece(pair * (KH // 2) + m // 2, m % 2, for_c=True)
                    store_h1(pair + 1, m)
                    store_piece(pair * (KH // 2) + m // 2, m % 2, for_c=True)
                load_bx(pair + 3)
            sp.wait_ge(piece_out, 16 * 8 * NB)
            for m in range(KH):
                sp.dma_start(wh2_hi[:, m, :].bitcast(F32), w_hi_d[m, :, H2_AT:W3_AT]).then_inc(wh2_in[m], 16)
            with sp.Fori(3, NB - 2) as b:
                for m in range(KH):
                    store_h1(b, m)
                load_bx(b + 2)
            for m in range(KH):
                store_h1(NB - 2, m)
            def load_wh2_lo(m):
                sp.dma_start(wh2_lo[m][:].bitcast(F32), w_lo_d[m, :, H2_AT:W3_AT]).then_inc(wh2_in[m], 16)

            def load_h1(b, k):
                wait_count(sp, h1_split, KH * b + k - 3)
                sp.dma_start(h1_in[k % 4][:], h1_d[b, :, k, :]).then_inc(h1_in_s[k % 4], 16)

            sp.wait_ge(up_done, KH * NB)
            sp.wait_ge(h0_split, KH * NB)
            for i in range(2):
                sp.wait_ge(h1_out[i], 16 * (NB - 1) * KH // 2)
            for k in range(4):
                load_h1(0, k)
            for m in range(KH // 2):
                load_wh2_lo(m)
            for m in range(KH):
                store_h1(NB - 1, m)
                if m + 4 < KH:
                    load_h1(0, m + 4)

            sp.dma_start(w3_hi[:].bitcast(F32), w_hi_d[:, :, W3_AT:PACK].rearrange("m p c -> p m c")).then_inc(w3_in, 16)
            sp.dma_start(w3_lo[:].bitcast(F32), w_lo_d[:, :, W3_AT:PACK].rearrange("m p c -> p m c")).then_inc(w3_in, 16)
            for m in range(KH // 2, KH):
                load_wh2_lo(m)
            for i in range(2):
                sp.wait_ge(h1_out[i], 16 * NB * KH // 2)

            def results_c(b):
                sp.wait_ge(y_ready, 2 * (b + 1))
                sp.dma_start(out_v[b], y_s[:]).then_inc(y_out, 16)

            def phase_c(b, par, first, last):
                for k in range(KH):
                    if not last:
                        load_h1(b + 1, k)
                    if k == 5:
                        if not first:
                            results_c(b - 1)
                        wait_count(sp, y_sum, 2 * b)
                        sp.dma_start(x1_s[:], x1_d[b]).then_inc(x1_in, 16)

            over_blocks(sp, phase_c)
            results_c(NB - 1)
            sp.wait_ge(y_out, 16 * (NB + 1))

        @block.tensor
        def _(pe):
            def qkv(b, t, kc):
                if t == 0:
                    pe.wait_ge(xT_ready, b + 1)
                if kc == 0:
                    wait_count(pe, qk_read, NT * b + t)
                    wait_count(pe, v_read, NT * b + t)
                xh = xT_hi[:, kc, t * P:(t + 1) * P]
                xl = xT_lo[:, kc, t * P:(t + 1) * P]
                for n, (a, w) in enumerate(((xh, wq_hi), (xh, wq_lo), (xl, wq_hi))):
                    first, last = kc == 0 and n == 0, kc == KD - 1 and n == 2
                    pe.matmul(ps_qk[:, :], a, w[:, kc, 0:2 * D], start=first, stop=last)
                    mm = pe.matmul(ps_v[:, 0:D], a, w[:, kc, 2 * D:3 * D], start=first, stop=last)
                if kc == KD - 1:
                    mm.then_inc(qkv_done, 1)

            def stack_transpose(b, g, in_turn=(ps_stack,)):
                t, part = STACK_ORDER[g]
                wait_count(pe, stackT_read, STEPS * b + g + 1 - len(in_turn))
                dst = in_turn[g % len(in_turn)][:, :].bitcast(F32R)
                pe.wait_ge(stack_lo, 2 * (NT * b + t + 1))
                pe.wait_ge(stack_hi2, 2 * (NT * b + t + 1))
                flat = stack[t % 2][:].rearrange("p h s d -> p (h s d)")
                at = (part % 2) * H * SLOT + (part // 2) * 4 * P
                for j in range(4):
                    mm = pe.transpose(dst[:, j * P:(j + 1) * P], flat[:, at + j * P:at + (j + 1) * P],
                                      ident_r[:, :])
                mm.then_inc(stackT_done, 1)

            def scores(b, par, s):
                hg, i = s // NT, s % NT
                if hg == 0:
                    pe.wait_ge(stackT_read, STEPS * b + STACKS_BEFORE_SCORES[i])
                elif s == 2 * NT:
                    pe.wait_ge(stackT_read, NST * NT * (b + 1))
                k0 = max(i - 1, 0) * P
                for j in range(2):
                    hp = 2 * hg + j
                    for r in range(2):
                        if j == 0:
                            wait_count(pe, merged, 2 * (STEPS * b + s - 1) + r + 1)
                        lo = SLOT * r
                        mm = pe.matmul(ps_score[r][:, j * 2 * P:(j + 1) * 2 * P],
                                       qT[par][lo:lo + PARTS, hp, i * P:(i + 1) * P],
                                       kT[par][lo:lo + PARTS, hp, k0:k0 + 2 * P], start=True, stop=True)
                        if j == 1:
                            mm.then_inc(score_done, 1)

            def prob_transpose(b, s):
                wait_count(pe, turned_ready, STEPS * b + s)
                pe.wait_ge(exp_done, STEPS * b + s + 1)
                for c in range(GH):
                    mm = pe.transpose(ps_probT[:, c * P:(c + 1) * P], prob[s % 2][:, c, :], ident_s[:, :])
                mm.then_inc(probT_done, 1)

            def weigh(b, par, s, j):
                hg = s // NT
                if j == 0:
                    wait_count(pe, head_read, NG * b + hg)
                n = 2 * P if j < NT - 1 else P
                for c in range(GH):
                    mm = pe.matmul(ps_head[32 * c:32 * c + 32, j * P:j * P + n], v_s[par][:, j, hg * GH + c, :],
                                   probT[j][:, c, 0:n], start=(j == 0), stop=(j == NT - 1),
                                   skip_group_check=True)
                mm.then_inc(head_done, 1)

            def weigh_behind(b, par, s):
                i = s % NT
                if i >= 1:
                    if i == 1:
                        pe.wait_ge(first_ready, NG * b + s // NT + 1)
                    else:
                        pe.wait_ge(lower_ready, later_tiles(b, s - 1))
                    pe.wait_ge(upper_ready, later_tiles(b, s))
                    weigh(b, par, s, i - 1)
                if i == NT - 1:
                    pe.wait_ge(lower_ready, later_tiles(b, s))
                    weigh(b, par, s, i)

            def to_tokens(b, hg, no):
                pe.wait_ge(head_read, NG * b + hg + 1)
                wait_count(pe, shared_read, no)
                for t in range(NT):
                    mm = pe.transpose(ps_shared[:, t * P:(t + 1) * P], headT[:, t * P:(t + 1) * P], ident_s[:, :])
                mm.then_inc(shared_done, 1)

            def turn(src, kc, no):
                pe.wait_ge(shared_read, no)
                for t in range(NT):
                    mm = pe.transpose(ps_shared[:, t * P:(t + 1) * P], src[:, t, kc * P:(kc + 1) * P], ident_s[:, :])
                mm.then_inc(shared_done, 1)

            def project(pair, no):
                pe.wait_ge(shared_read, no)
                n = 0
                for u in range(2):
                    t = 2 * pair + u
                    for kc in range(KD):
                        ah, al = (a[:, kc, t * P:(t + 1) * P] for a in (attT_hi, attT_lo))
                        for a, w in ((ah, wo_hi), (ah, wo_lo), (al, wo_hi)):
                            mm = pe.matmul(ps_shared[:, u * D:(u + 1) * D], a, w[:, kc, :], start=(n == 0),
                                           stop=(n % 6 == 5), skip_group_check=True)
                            n += 1
                mm.then_inc(shared_done, 1)

            def shared(b, s, first, flush):
                if not uses_shared(s, first, flush):
                    return
                no = shared_uses(b, s, first, flush)
                if s in TO_TOKENS:
                    back, hg = TO_TOKENS[s]
                    to_tokens(b + back, hg, no)
                elif s in (5, 6):
                    turn(att, s - 5, no)
                elif s in (9, 10):
                    project(s - 9, no)
                else:
                    if s == 14:
                        pe.wait_ge(x1_ready, 2 * b)
                    turn(res, s - 14, no)

            def phase_a(b, par, first, last):
                for s in range(STEPS):
                    scores(b, par, s)
                    if s >= 2:
                        prob_transpose(b, s - 2)
                    elif not first:
                        prob_transpose(b - 1, s - 2 + STEPS)
                    if s in STACK_STEP and not last:
                        stack_transpose(b + 1, STACK_STEP[s])
                    if s in LATE_STACK:
                        stack_transpose(b, LATE_STACK[s])
                    for kc in range(KD):
                        if s + 1 - kc in QKV_STEP and not last:
                            qkv(b + 1, QKV_STEP[s + 1 - kc], kc)
                    if s >= 4:
                        weigh_behind(b, par, s - 4)
                    elif not first:
                        weigh_behind(b - 1, 1 - par, s - 4 + STEPS)
                    shared(b, s, first, False)

            def split_products(acc, w_hi, w_lo, a_hi, a_lo, start, stop):
                pe.matmul(acc, w_hi, a_hi, start=start, stop=False)
                pe.matmul(acc, w_hi, a_lo, start=False, stop=False)
                return pe.matmul(acc, w_lo, a_hi, start=False, stop=stop)

            def glu(b, m, up):
                acc, done, read = (ps_up, up_done, h0_ready) if up else (ps_gate, gate_done, silu_ready)
                wait_count(pe, read, KH * b + m - 1)
                for kc in range(KD):
                    at = (up * KD + kc) * P
                    mm = split_products(acc[m % 2][:, :], wglu_hi[:, m, at:at + P], wglu_lo[:, m, at:at + P],
                                        bx_hi[:, kc, :], bx_lo[:, kc, :], kc == 0, kc == KD - 1)
                mm.then_inc(done, 1)

            def first_layer(b, first):
                for m in range(KH):
                    if first:
                        pe.wait_ge(wh1_in[m], 32)
                    wait_count(pe, h1_ready, KH * b + m - 1)
                    for k in range(KH):
                        if m == 0:
                            pe.wait_ge(h0_split, KH * b + k + 1)
                        mm = split_products(ps_h[m % 2][:, :], wh1_hi[:, m, k * P:(k + 1) * P],
                                            wh1_lo[:, m, k * P:(k + 1) * P], h0_hi[:, k, :], h0_lo[:, k, :],
                                            k == 0, k == KH - 1)
                    mm.then_inc(h1_mm, 1)

            for kc in range(KD):
                pe.wait_ge(wattn_split, kc + 1)
                qkv(0, 0, kc)
            pe.wait_ge(const_set, 7)
            for t in range(1, NT):
                for kc in range(KD):
                    qkv(0, t, kc)
                for g in range(NST * (t - 1), min(NST * t, LATE_STACK[0])):
                    stack_transpose(0, g, SETUP_BANKS)
            pe.wait_ge(wattn_split, 3)
            over_blocks(pe, phase_a)
            pe.wait_ge(bx_ready, 1)
            pe.wait_ge(qk_read, NT * NB)
            pe.wait_ge(v_read, NT * NB)
            pe.wait_ge(merged, 2 * STEPS * NB)
            for s in range(FLUSH_STEPS):
                if s % 2 == 0:
                    pe.wait_ge(wglu_in[s // 2], 32)
                glu(0, s // 2, s % 2)
                if s < 2:
                    prob_transpose(NB - 1, s - 2 + STEPS)
                if s < 4:
                    weigh_behind(NB - 1, 1, s - 4 + STEPS)
                shared(NB, s, False, True)

            pe.wait_ge(shared_read, shared_uses(NB, 15, False, True) + 1)
            first_layer(0, True)
            with pe.Fori(1, NB) as b:
                pe.wait_ge(bx_ready, b + 1)
                for m in range(KH):
                    for up in range(2):
                        glu(b, m, up)
                first_layer(b, False)

            pe.wait_ge(h0_ready, KH * NB)

            def third(b, m):
                pe.wait_ge(h2_split, KH * b + m + 1)
                if m == 0:
                    wait_count(pe, oT_ready, KD * b)
                for kc in range(KD):
                    mm = split_products(ps_oT[kc][:, :], w3_hi[:, m, kc * P:(kc + 1) * P],
                                        w3_lo[:, m, kc * P:(kc + 1) * P], h2_hi[m % 2][:, :], h2_lo[m % 2][:, :],
                                        m == 0, m == KH - 1)
                mm.then_inc(w3_done, 1)

            def to_rows(b):
                pe.wait_ge(oT_ready, KD * (b + 1))
                wait_count(pe, y_sum, 2 * b)
                for pair in range(2):
                    for u in range(2):
                        t = 2 * pair + u
                        for kc in range(KD):
                            mm = pe.transpose(ps_y[pair][:, u * D + kc * P:u * D + (kc + 1) * P],
                                              oT_s[:, kc, t * P:(t + 1) * P], ident_s[:, :])
                    mm.then_inc(yT_done, 1)

            def phase_c(b, par, first, last):
                for m in range(KH):
                    if first:
                        pe.wait_ge(wh2_in[m], 32)
                    if first and m < 2:
                        pe.wait_ge(h1_ready, KH * NB - 1 + m)
                    wait_count(pe, h2_ready, KH * b + m - 1)
                    for k in range(KH):
                        if m == 0:
                            pe.wait_ge(h1_split, KH * b + k + 1)
                        mm = split_products(ps_h[m % 2][:, :], wh2_hi[:, m, k * P:(k + 1) * P],
                                            wh2_lo[m][:, k * P:(k + 1) * P], h1_hi[par][:, k, :],
                                            h1_lo[par][:, k, :], k == 0, k == KH - 1)
                    mm.then_inc(h2_mm, 1)
                    if first and m == 1:
                        pe.wait_ge(w3_in, 16 * 2)
                    if m >= 1:
                        third(b, m - 1)
                    elif not first:
                        third(b - 1, KH - 1)
                    if m == 1 and not first:
                        to_rows(b - 1)

            over_blocks(pe, phase_c)
            third(NB - 1, KH - 1)
            to_rows(NB - 1)

        @block.scalar
        def _(act):
            def stage_v(b, par, t):
                act.wait_ge(qkv_done, NT * b + t + 1)
                wait_count(act, head_done, STEPS * (b - 1) - NT + t + 1)
                act.activation(v_s[par][:, t, :, 0:HD], ps_v[:, 0:D].rearrange("p (h d) -> p h d", d=HD),
                               ACT.Copy).then_inc(v_read, 1)

            def stack_out(b, par, g, in_turn=(ps_stack,)):
                t, part = STACK_ORDER[g]
                dst = (qT, kT)[part % 2][par]
                act.wait_ge(stackT_done, NST * NT * b + g + 1)
                if g == 0:
                    wait_count(act, score_done, 2 * STEPS * (b - 1))
                act.activation(dst[:, 4 * (part // 2):4 * (part // 2) + 4, t * P:(t + 1) * P],
                               in_turn[g % len(in_turn)][:, :].rearrange("p (j n) -> p j n", n=P),
                               ACT.Copy).then_inc(stackT_read, 1)

            def copy_scores(b, s):
                for r in range(2):
                    act.wait_ge(score_done, 2 * (STEPS * b + s) + r + 1)
                    wait_count(act, exp_done, STEPS * b + s - 1)
                    act.activation(merged_s[s % 2][:, r::2, :],
                                   ps_score[r][:, :].rearrange("p (h n) -> p h n", h=2)[:, :, P:2 * P],
                                   ACT.Copy).then_inc(copied, 1)

            def exponentials(b, s):
                act.wait_ge(low_ready, STEPS * b + s + 1)
                wait_count(act, probT_done, STEPS * b + s - 1)
                for c in range(GH):
                    a = act.activation(prob[s % 2][:, c, :], merged_s[s % 2][:, c, :], ACT.Exp,
                                       bias=low[s % 2][:, c:c + 1], scale=-1.0)
                a.then_inc(exp_done, 1)

            def turned_out(b, s):
                act.wait_ge(probT_done, STEPS * b + s + 1)
                if (s - 2) % NT == 0:
                    wait_count(act, first_ready, NG * b + (s - 2) // NT + 1)
                else:
                    wait_count(act, lower_ready, later_tiles(b, s - 2))
                    wait_count(act, upper_ready, later_tiles(b, s - 2))
                act.activation(turned[s % 2][:].rearrange("p c n -> p (c n)"), ps_probT[:, :],
                               ACT.Copy).then_inc(turned_ready, 1)

            def head_out(b, s, first, flush):
                if s not in TO_TOKENS or not uses_shared(s, first, flush):
                    return
                back, hg = TO_TOKENS[s]
                act.wait_ge(head_done, STEPS * (b + back) + NT * hg + NT)
                if s == 0:
                    act.wait_ge(shared_done, shared_uses(b, 0, first, flush))
                elif uses_shared(s - NT, first, flush):
                    act.wait_ge(shared_done, shared_uses(b, s - NT, first, flush) + 1)
                act.activation(headT[:, :], ps_head[:, :], ACT.Copy).then_inc(head_read, 1)

            def shared(b, s, first, flush):
                if first or s not in (5, 6, 14, 15):
                    return
                act.wait_ge(shared_done, shared_uses(b, s, first, flush) + 1)
                if s in (5, 6):
                    act.activation(attT_hi[:, s - 5, :], ps_shared[:, :], ACT.Copy).then_inc(shared_hi, 1)
                else:
                    if s == 14:
                        act.wait_ge(x1T_out, 16 * b)
                    act.activation(x1T_s[:, s - 14, :], ps_shared[:, :], ACT.Copy).then_inc(shared_read, 1)

            def phase_a(b, par, first, last):
                for s in range(STEPS):
                    if s % NT:
                        copy_scores(b, s)
                    if s >= 1:
                        exponentials(b, s - 1)
                    elif not first:
                        exponentials(b - 1, s - 1 + STEPS)
                    head_out(b, s, first, False)
                    if s in STACK_STEP and not last:
                        stack_out(b + 1, 1 - par, STACK_STEP[s])
                    if s in LATE_STACK:
                        stack_out(b, par, LATE_STACK[s])
                    if s >= 2:
                        turned_out(b, s - 2)
                    elif not first:
                        turned_out(b - 1, s - 2 + STEPS)
                    if s in QKV_STEP and not last:
                        stage_v(b + 1, 1 - par, QKV_STEP[s])
                    shared(b, s, first, False)
                    if last and s == 12:
                        split_bx(0)

            def split_bx(b):
                act.wait_ge(bx_in, 16 * (b + 1))
                wait_count(act, up_done, KH * b)
                act.activation(bx_hi[:], bx_s[:], ACT.Copy).then_inc(bx_hi_ready, 1)

            def h0_high(b, m):
                act.wait_ge(h0_ready, KH * b + m + 1)
                wait_count(act, h1_mm, KH * b)
                act.activation(h0_hi[:, m, :], h0_s[m % 2][:], ACT.Copy).then_inc(h0_hi_ready, 1)

            def gate(b, m):
                act.wait_ge(gate_done, KH * b + m + 1)
                wait_count(act, h0_ready, KH * b + m - 1)
                act.activation(silu_s[m % 2][:], ps_gate[m % 2][:, :], ACT.Silu,
                               scale=s1_s[:, m:m + 1]).then_inc(silu_ready, 1)
                if m:
                    h0_high(b, m - 1)

            act.wait_ge(wattn_in[0], 16)
            act.activation(wq_hi[:, 0], wq_f[:, 0], ACT.Copy).then_inc(wattn_hi, 1)
            act.wait_ge(wattn_in[1], 16)
            act.activation(wq_hi[:, 1], wq_f[:, 1], ACT.Copy).then_inc(wattn_hi, 1)
            act.wait_ge(wattn_in[2], 16)
            act.activation(wo_hi[:], wo_f[:], ACT.Copy).then_inc(wattn_hi, 1)
            for t in range(NT):
                stage_v(0, 0, t)
                for g in range(max(NST * (t - 1), 0), min(NST * t, LATE_STACK[0])):
                    stack_out(0, 0, g, SETUP_BANKS)
            over_blocks(act, phase_a)
            for s in range(FLUSH_STEPS):
                if s % 2 == 1:
                    gate(0, s // 2)
                if s == 0:
                    exponentials(NB - 1, STEPS - 1)
                if s < 2:
                    turned_out(NB - 1, s - 2 + STEPS)
                head_out(NB, s, False, True)
                shared(NB, s, False, True)

            def split_h1(b, par, k):
                act.wait_ge(h1_in_s[k % 4], 16 * (KH // 4 * b + k // 4 + 1))
                wait_count(act, h2_mm, KH * (b - 1))
                act.activation(h1_hi[par][:, k, :], h1_in[k % 4][:], ACT.Copy).then_inc(h1_hi_ready, 1)

            def gelu_first(b, last):
                for m in range(KH):
                    act.wait_ge(h1_mm, KH * b + m + 1)
                    wait_count(act, h1_out[m % 2], 16 * (KH // 2 * b + m // 2))
                    act.activation(h1_s[m % 2][:], ps_h[m % 2][:, :], ACT.Gelu,
                                   scale=sh1_s[:, m:m + 1]).then_inc(h1_ready, 1)
                    if m == 1 and not last:
                        split_bx(b + 1)
                    if last:
                        split_h1(0, 0, m)

            def phase_b(b, last):
                for m in range(KH):
                    gate(b, m)
                h0_high(b, KH - 1)
                gelu_first(b, last)

            h0_high(0, KH - 1)
            gelu_first(0, False)
            with act.Fori(1, NB - 1) as b:
                phase_b(b, False)
            phase_b(NB - 1, True)

            def out_features(b):
                act.wait_ge(w3_done, KH * (b + 1))
                for kc in range(KD):
                    act.activation(oT_s[:, kc, :], ps_oT[kc][:, :], ACT.Copy,
                                   scale=s3_s[:, kc:kc + 1]).then_inc(oT_ready, 1)

            def phase_c(b, par, first, last):
                for m in range(KH):
                    act.wait_ge(h2_mm, KH * b + m + 1)
                    wait_count(act, h2_split, KH * b + m - 1)
                    act.activation(h2_s[m % 2][:], ps_h[m % 2][:, :], ACT.Gelu,
                                   scale=sh2_s[:, m:m + 1]).then_inc(h2_ready, 1)
                    act.wait_ge(h2_ready, KH * b + m + 1)
                    wait_count(act, w3_done, KH * b + m - 1)
                    act.activation(h2_hi[m % 2][:], h2_s[m % 2][:], ACT.Copy).then_inc(h2_hi_ready, 1)
                    if m == 0 and not first:
                        out_features(b - 1)
                    if not last:
                        split_h1(b + 1, 1 - par, m)

            over_blocks(act, phase_c)
            out_features(NB - 1)

        @block.vector
        def _(dve):
            def split_x(b):
                dve.wait_ge(xT_in, 16 * (b + 1))
                wait_count(dve, qkv_done, NT * b)
                dve.tensor_copy(xT_hi[:], xT_s[:]).then_inc(xT_hi_ready, 1)

            for kc in range(KD):
                if kc == 1:
                    split_x(0)
                    dve.wait_ge(xT_hi_ready, 1)
                    dve.tensor_tensor(xT_lo[:], xT_s[:], xT_hi[:].bitcast(F32), ALU.subtract).then_inc(xT_ready, 1)
                dve.wait_ge(wattn_hi, kc + 1)
                dve.tensor_tensor(wq_lo[:, kc], wq_f[:, kc], wq_hi[:, kc].bitcast(F32),
                                  ALU.subtract).then_inc(wattn_split, 1)
            dve.memset(neg_half[:], -0.5).then_inc(const_set, 1)
            for st in stack:
                dve.memset(st[:, :, 3, :].bitcast(F32), 0.0).then_inc(const_set, 1)
            for v in v_s:
                dve.memset(v[:, :, :, HD:2 * HD], 1.0).then_inc(const_set, 1)
            dve.wait_ge(const_in, 16 * N_CONST)
            dve.tensor_copy(ident_r[:], ident_s[:]).then_inc(const_set, 1)
            dve.tensor_scalar(take_s[:], bias_s[:], 1.0, None, ALU.is_gt).then_inc(const_set, 1)
            dve.wait_ge(const_set, 7)

            def stage_hi(b, t):
                dve.wait_ge(rope_sum, NT * b + t + 1)
                wait_count(dve, stackT_done, STEPS * (b - (t < 2)) + STACKS_OF_TILE[t - 2])
                st = stack[t % 2]
                src = qk_s[t % 2][:].rearrange("p (h d) -> p h d", d=HD)
                dve.tensor_copy(st[:, :, 0, :], src).then_inc(stack_hi, 1)
                dve.tensor_copy(st[:, 0:H, 1, :], src[:, 0:H, :]).then_inc(stack_hi2, 1)
                dve.tensor_copy(st[:, H:2 * H, 2, :], src[:, H:2 * H, :]).then_inc(stack_hi2, 1)

            def rope(b, t):
                dve.wait_ge(qkv_done, NT * b + t + 1)
                wait_count(dve, rope_sum, NT * b + t)
                x4 = ps_qk[:, :].rearrange("p (q h d) -> p q h d", q=2, d=HD)
                b4 = rope_b[:].rearrange("p (q h d) -> p q h d", q=2, d=HD)
                a3 = rope_a[:].rearrange("p (q g e) -> p q g e", q=2, e=HALF)
                x3 = ps_qk[:, :].rearrange("p (q g e) -> p q g e", q=2, e=HALF)
                dve.tensor_tensor(a3, x3, cos_s[:, t].unsqueeze(2).broadcast_to([P, 2, 2 * H, HALF]),
                                  ALU.mult).then_inc(rope_terms, 1)
                dve.tensor_tensor(b4[:, :, :, 0:HALF], x4[:, :, :, HALF:HD],
                                  nsin_s[:, t].unsqueeze(2).broadcast_to([P, 2, H, HALF]),
                                  ALU.mult).then_inc(rope_terms, 1)
                dve.tensor_tensor(b4[:, :, :, HALF:HD], x4[:, :, :, 0:HALF],
                                  sin_s[:, t].unsqueeze(2).broadcast_to([P, 2, H, HALF]),
                                  ALU.mult).then_inc(qk_read, 1)

            def merge(b, s):
                for r in range(2):
                    dst = merged_s[s % 2][:, r::2, :]
                    src = ps_score[r][:, :].rearrange("p (h n) -> p h n", h=2)[:, :, 0:P]
                    if s % NT == 0:
                        dve.wait_ge(score_done, 2 * (STEPS * b + s) + r + 1)
                        wait_count(dve, exp_done, STEPS * b + s - 1)
                        dve.tensor_tensor(dst, src, bias_s[:].unsqueeze(1).broadcast_to([P, 2, P]),
                                          ALU.add).then_inc(merged, 1)
                    else:
                        dve.wait_ge(copied, 2 * (NT - 1) * (NG * b + s // NT) + 2 * (s % NT - 1) + r + 1)
                        dve.nop(nofuse=True)
                        dve.copy_predicated(dst, take_s[:].unsqueeze(1).broadcast_to([P, 2, P]),
                                            src).then_inc(merged, 1)
                dve.wait_ge(merged, 2 * (STEPS * b + s) + 2)
                wait_count(dve, exp_done, STEPS * b + s - 1)
                dve.tensor_reduce(low[s % 2][:], merged_s[s % 2][:], AX.X, ALU.min).then_inc(low_ready, 1)

            def lower_probs(b, s):
                if s % NT == 0:
                    return
                dve.wait_ge(turned_ready, STEPS * b + s + 1)
                wait_count(dve, head_done, STEPS * b + s - NT + 1)
                dve.tensor_tensor(probT[s % NT][:, :, 0:P], turned[s % 2][:],
                                  lower_s[:].unsqueeze(1).broadcast_to([P, GH, P]), ALU.mult).then_inc(lower_ready, 1)

            def normalise(b, hg, no):
                dve.wait_ge(shared_done, no + 1)
                sums = ps_shared[:, :].rearrange("p (t c e) -> p t c e", c=GH, e=2 * HD)
                dve.reciprocal(denom[:], sums[:, :, :, HD]).then_inc(denom_ready, 1)
                dve.wait_ge(denom_ready, NG * b + hg + 1)
                dst = att[:].rearrange("p t (g c d) -> p t g c d", g=NG, d=HD)[:, :, hg]
                dve.tensor_tensor(dst, sums[:, :, :, 0:HD], denom[:].unsqueeze(3).broadcast_to([P, NT, GH, HD]),
                                  ALU.mult).then_inc(shared_read, 1)

            def residual(b, par, pair, no):
                dve.wait_ge(shared_done, no + 1)
                if pair == 0:
                    dve.wait_ge(x_in, 16 * (b + 1))
                    dve.wait_ge(x1_out, 16 * (b + 1))
                r = res[:, 2 * pair:2 * pair + 2, :]
                dve.tensor_tensor(r, ps_shared[:, :].rearrange("p (t d) -> p t d", t=2),
                                  x_s[par][:, 2 * pair:2 * pair + 2, :], ALU.add).then_inc(shared_read, 1)
                dve.wait_ge(shared_read, no + 1)
                statistics(res, pair, b, stats_ready, mean_ready)

            def statistics(src, pair, b, stats_sem, mean_sem):
                for u in range(2):
                    dve.bn_stats(stats[:, 2 * pair + u, :], src[:, 2 * pair + u, :]).then_inc(stats_sem, 1)
                dve.wait_ge(stats_sem, 2 * (2 * b + pair) + 2)
                dve.nop(nofuse=True)
                for u in range(2):
                    dve.bn_aggr(meanvar[:, 2 * pair + u, :], stats[:, 2 * pair + u, :]).then_inc(mean_sem, 1)

            def normed(src, dst, pair, b, rstd_sem, ready):
                dve.wait_ge(rstd_sem, 2 * b + pair + 1)
                for u in range(2):
                    t = 2 * pair + u
                    op = dve.tensor_scalar(dst[:, t, :], src[:, t, :], meanvar[:, t, 0:1], rstd[:, t:t + 1],
                                           ALU.subtract, ALU.mult)
                op.then_inc(ready, 1)

            def shared(b, par, s, first, flush):
                if not uses_shared(s, first, flush):
                    return
                no = shared_uses(b, s, first, flush)
                if s in TO_TOKENS:
                    back, hg = TO_TOKENS[s]
                    normalise(b + back, hg, no)
                elif s in (5, 6):
                    dve.wait_ge(shared_hi, KD * (b - 1) + s - 4)
                    dve.tensor_tensor(attT_lo[:, s - 5, :], ps_shared[:, :], attT_hi[:, s - 5, :].bitcast(F32),
                                      ALU.subtract).then_inc(shared_read, 1)
                elif s in (9, 10):
                    residual(b - 1, 1 - par, s - 9, no)

            def phase_a(b, par, first, last):
                for s in range(STEPS):
                    if s == 0 and not last:
                        split_x(b + 1)
                    merge(b, s)
                    if s >= 3:
                        lower_probs(b, s - 3)
                    elif not first:
                        lower_probs(b - 1, s - 3 + STEPS)
                    if s in (12, 13) and not first:
                        normed(res, res, s - 12, b - 1, rstd_ready, x1_ready)
                    if s - 1 in QKV_STEP and not last:
                        rope(b + 1, QKV_STEP[s - 1])
                    if s - 2 in QKV_STEP and not last:
                        stage_hi(b + 1, QKV_STEP[s - 2])
                    shared(b, par, s, first, False)
                    if last and s == 13:
                        split_bx(0)

            def split_bx(b):
                dve.wait_ge(bx_hi_ready, b + 1)
                dve.tensor_tensor(bx_lo[:], bx_s[:], bx_hi[:].bitcast(F32), ALU.subtract).then_inc(bx_ready, 1)

            def h0_low(b, m):
                dve.wait_ge(h0_hi_ready, KH * b + m + 1)
                dve.tensor_tensor(h0_lo[:, m, :], h0_s[m % 2][:], h0_hi[:, m, :].bitcast(F32),
                                  ALU.subtract).then_inc(h0_split, 1)

            def gating(b, m):
                dve.wait_ge(up_done, KH * b + m + 1)
                dve.wait_ge(silu_ready, KH * b + m + 1)
                wait_count(dve, h0_split, KH * b + m - 1)
                dve.scalar_tensor_tensor(h0_s[m % 2][:], ps_up[m % 2][:, :], s2_s[:, m:m + 1],
                                         silu_s[m % 2][:], ALU.mult, ALU.mult).then_inc(h0_ready, 1)
                if m:
                    h0_low(b, m - 1)

            dve.wait_ge(wattn_hi, 3)
            dve.tensor_tensor(wo_lo[:], wo_f[:], wo_hi[:].bitcast(F32), ALU.subtract).then_inc(wattn_split, 1)
            for t in range(NT):
                rope(0, t)
                stage_hi(0, t)
            over_blocks(dve, phase_a)
            for s in range(FLUSH_STEPS):
                if s < 3:
                    lower_probs(NB - 1, s - 3 + STEPS)
                if s in (12, 13):
                    normed(res, res, s - 12, NB - 1, rstd_ready, x1_ready)
                shared(NB, 0, s, False, True)
                if s % 2 == 1:
                    gating(0, s // 2)

            h0_low(0, KH - 1)
            split_bx(1)
            with dve.Fori(1, NB - 1) as b:
                for m in range(KH):
                    gating(b, m)
                h0_low(b, KH - 1)
                split_bx(b + 1)
            for m in range(KH):
                gating(NB - 1, m)
            h0_low(NB - 1, KH - 1)

            def split_h1(b, par, k):
                dve.wait_ge(h1_hi_ready, KH * b + k + 1)
                dve.tensor_tensor(h1_lo[par][:, k, :], h1_in[k % 4][:], h1_hi[par][:, k, :].bitcast(F32),
                                  ALU.subtract).then_inc(h1_split, 1)

            def out_rows(b, pair):
                dve.wait_ge(yT_done, 2 * b + pair + 1)
                if pair == 0:
                    dve.wait_ge(x1_in, 16 * (b + 1))
                    dve.wait_ge(y_out, 16 * (b + 1))
                dve.tensor_tensor(y_s[:, 2 * pair:2 * pair + 2, :], ps_y[pair][:, :].rearrange("p (t d) -> p t d", t=2),
                                  x1_s[:, 2 * pair:2 * pair + 2, :], ALU.add).then_inc(y_sum, 1)
                dve.wait_ge(y_sum, 2 * b + pair + 1)
                statistics(y_s, pair, b, cstats_ready, cmean_ready)

            def phase_c(b, par, first, last):
                for m in range(KH):
                    dve.wait_ge(h2_hi_ready, KH * b + m + 1)
                    dve.tensor_tensor(h2_lo[m % 2][:], h2_s[m % 2][:], h2_hi[m % 2][:].bitcast(F32),
                                      ALU.subtract).then_inc(h2_split, 1)
                    if not last:
                        split_h1(b + 1, 1 - par, m)
                    if not first and m in (1, 2):
                        out_rows(b - 1, m - 1)
                    if not first and m in (3, 4):
                        normed(y_s, y_s, m - 3, b - 1, crstd_ready, y_ready)

            for k in range(KH):
                split_h1(0, 0, k)
            over_blocks(dve, phase_c)
            for pair in range(2):
                out_rows(NB - 1, pair)
            for pair in range(2):
                normed(y_s, y_s, pair, NB - 1, crstd_ready, y_ready)

        @block.gpsimd
        def _(pool):
            def split_x(b):
                pool.wait_ge(xT_hi_ready, b + 1)
                pool.tensor_tensor(xT_lo[:], xT_s[:], xT_hi[:].bitcast(F32), ALU.subtract).then_inc(xT_ready, 1)

            def rotate(b, t):
                pool.wait_ge(rope_terms, 2 * (NT * b + t + 1))
                pool.wait_ge(qk_read, NT * b + t + 1)
                wait_count(pool, stack_hi2, 2 * (NT * b + t - 1))
                wait_count(pool, stack_lo, 2 * (NT * b + t - 1))
                pool.tensor_tensor(qk_s[t % 2][:], rope_a[:], rope_b[:], ALU.add).then_inc(rope_sum, 1)

            def upper_probs(b, s):
                pool.wait_ge(turned_ready, STEPS * b + s + 1)
                if s % NT == 0:
                    wait_count(pool, head_done, STEPS * b + s - NT + 1)
                    pool.tensor_tensor(probT[0][:, :, 0:P], turned[s % 2][:],
                                       lower_s[:].unsqueeze(1).broadcast_to([P, GH, P]),
                                       ALU.mult).then_inc(first_ready, 1)
                    return
                wait_count(pool, head_done, STEPS * b + s - NT)
                pool.tensor_tensor(probT[s % NT - 1][:, :, P:2 * P], turned[s % 2][:],
                                   upper_s[:].unsqueeze(1).broadcast_to([P, GH, P]),
                                   ALU.mult).then_inc(upper_ready, 1)

            def stack_low(b, t):
                st = stack[t % 2]
                src = qk_s[t % 2][:].rearrange("p (h d) -> p h d", d=HD)
                pool.wait_ge(stack_hi, NT * b + t + 1)
                pool.tensor_tensor(st[:, 0:H, 2, :], src[:, 0:H, :], st[:, 0:H, 0, :].bitcast(F32),
                                   ALU.subtract).then_inc(stack_lo, 1)
                pool.tensor_tensor(st[:, H:2 * H, 1, :], src[:, H:2 * H, :], st[:, H:2 * H, 0, :].bitcast(F32),
                                   ALU.subtract).then_inc(stack_lo, 1)

            def split_piece(done, q, half, n):
                cols = slice(half * n // 2, (half + 1) * n // 2)
                pool.wait_ge(piece_in[q], 16 * (done + 1))
                if half == 0:
                    wait_count(pool, piece_out, 32 * (2 * done + q))
                pool.nop(nofuse=True)
                pool.tensor_scalar(piece_hi[:, cols], piece[q][:, cols], 1.0, 1.0, ALU.mult,
                                   ALU.mult).then_inc(piece_hi_ready, 1)
                pool.wait_ge(piece_hi_ready, 4 * done + 2 * q + half + 1)
                pool.tensor_tensor(piece_lo[:, cols], piece[q][:, cols], piece_hi[:, cols].bitcast(F32),
                                   ALU.subtract).then_inc(piece_lo_ready, 1)

            def inverse_deviation(b, pair, mean_sem, step, ready):
                n = 5 * (2 * b + pair)
                ab = slice(2 * pair, 2 * pair + 2)
                v, y, t, r = vareps[:, ab], rstd0[:, ab], rsq[:, ab], rstd[:, ab]
                pool.wait_ge(mean_sem, 2 * (2 * b + pair) + 2)
                pool.nop(nofuse=True)
                pool.tensor_scalar(v, meanvar[:, ab, 1], EPS, None, ALU.add).then_inc(step, 1)
                pool.wait_ge(step, n + 1)
                pool.tensor_tensor(y, v, neg_half[:, ab], ALU.pow).then_inc(step, 1)
                pool.wait_ge(step, n + 2)
                pool.tensor_tensor(t, y, y, ALU.mult).then_inc(step, 1)
                pool.wait_ge(step, n + 3)
                pool.tensor_tensor(t, t, v, ALU.mult).then_inc(step, 1)
                pool.wait_ge(step, n + 4)
                pool.nop(nofuse=True)
                pool.tensor_scalar(t, t, -0.5, 1.5, ALU.mult, ALU.add).then_inc(step, 1)
                pool.wait_ge(step, n + 5)
                pool.tensor_tensor(r, y, t, ALU.mult).then_inc(ready, 1)

            def phase_a(b, par, first, last):
                for s in range(STEPS):
                    if s == 0 and not last:
                        split_x(b + 1)
                    if s >= 3:
                        upper_probs(b, s - 3)
                    elif not first:
                        upper_probs(b - 1, s - 3 + STEPS)
                    if s in (10, 11) and not first:
                        inverse_deviation(b - 1, s - 10, mean_ready, rstd_step, rstd_ready)
                    if s - 1 in QKV_STEP and not last:
                        rotate(b + 1, QKV_STEP[s - 1])
                    if s - 2 in QKV_STEP and not last:
                        stack_low(b + 1, QKV_STEP[s - 2])
                    if s in PIECE_STEP:
                        split_piece(b, *PIECE_STEP[s], PIECE_B)

            for t in range(NT):
                rotate(0, t)
                stack_low(0, t)
            pool.wait_ge(const_in, 16 * N_CONST)
            over_blocks(pool, phase_a)
            for s in range(3):
                upper_probs(NB - 1, s - 3 + STEPS)
            for pair in range(2):
                inverse_deviation(NB - 1, pair, mean_ready, rstd_step, rstd_ready)
            with pool.Fori(NB, 2 * NB) as done:
                for q in range(2):
                    for half in range(2):
                        split_piece(done, q, half, PIECE_C)
            with pool.Fori(0, NB) as b:
                for pair in range(2):
                    inverse_deviation(b, pair, cmean_ready, crstd_step, crstd_ready)


def constants():
    theta = (1.0 / 10000.0 ** (np.arange(HALF, dtype=np.float32) / HALF)).astype(np.float32)
    freqs = np.arange(TB, dtype=np.float32)[:, None] * theta[None, :]
    by_tile = lambda a: np.ascontiguousarray(a.reshape(NT, P, HALF).transpose(1, 0, 2))
    scale = np.array([-1.0 / np.sqrt(HD), 1.0], np.float32)[None, None, :, None]
    cos = by_tile(np.cos(freqs).astype(np.float32))[:, :, None, :] * scale
    sin = by_tile(np.sin(freqs).astype(np.float32))[:, :, None, :] * scale
    row, col = np.arange(P)[:, None], np.arange(P)[None, :]
    return {
        "cos": cos,
        "sin": np.stack([sin, -sin]),
        "lower": (row <= col).astype(np.float32),
        "upper": (row > col).astype(np.float32),
        "bias": np.where(col > row, np.float32(MASKED), np.float32(0)),
        "ident": np.eye(P, dtype=np.float32),
    }


def kernel(**inputs):
    import concourse.bacc as bacc
    from concourse.bass_utils import run_bass_kernel_spmd

    a = {k.removeprefix("L0_"): np.asarray(v) for k, v in inputs.items()}
    flat = a["attn_x"].reshape(NB * TB, D)

    def chunks(w, k):
        return w.reshape(-1, P, k, P).transpose(0, 3, 2, 1)

    packed = np.concatenate(
        [chunks(a["ffn_w1_w"], KD).reshape(KH, P, -1), chunks(a["ffn_w2_w"], KD).reshape(KH, P, -1),
         chunks(a["ffn_h1_w"], KH).reshape(KH, P, -1), chunks(a["ffn_h2_w"], KH).reshape(KH, P, -1),
         a["ffn_w3_w"].T.reshape(KH, P, D)], axis=2)
    by_chunk = lambda s: s.reshape(-1, P).T
    arrays = {
        "x": flat,
        "xT": flat.reshape(NB, TB, KD, P).transpose(0, 3, 2, 1),
        "wqkv": a["attn_Wqkv"].reshape(KD, P, 3 * D).transpose(1, 0, 2),
        "wout": a["attn_Wout"].reshape(KD, P, D).transpose(1, 0, 2),
        "wffn": packed,
        "s1": by_chunk(a["ffn_w1_s"]), "s2": by_chunk(a["ffn_w2_s"]),
        "sh1": by_chunk(a["ffn_h1_s"]), "sh2": by_chunk(a["ffn_h2_s"]), "s3": by_chunk(a["ffn_w3_s"]),
    } | constants()
    nc = bacc.Bacc("TRN2", target_bir_lowering=False, num_devices=1)
    feed, args = {}, {}
    for name, array in arrays.items():
        array = np.ascontiguousarray(array)
        feed[f"in_{name}"] = array
        args[name] = nc.dram_tensor(f"in_{name}", array.shape, mybir.dt.from_np(array.dtype), kind="ExternalInput").ap()
    out = nc.dram_tensor("out_0", (NB * TB, D), F32, kind="ExternalOutput").ap()
    build(nc, out=out, **args)
    r = run_bass_kernel_spmd(nc, [feed], core_ids=[0])
    return r.results[0]["out_0"].reshape(NB, TB, D)
```
